# Optimizing a Trainium2 kernel written in Bass

```python
import numpy as np
import jax
import jax.numpy as jnp

def _softmax(x, axis=-1):
    return jax.nn.softmax(x, axis=axis)

def _gelu(x):
    return jax.nn.gelu(x, approximate=True)

def _silu(x):
    return jax.nn.silu(x)

def _sigmoid(x):
    return jax.nn.sigmoid(x)

def _layernorm(x, axis=-1, eps=1e-05):
    m = jnp.mean(x, axis=axis, keepdims=True)
    v = jnp.var(x, axis=axis, keepdims=True)
    return (x - m) / jnp.sqrt(v + eps)

def _scatter_add(tgt, idx, src, axis=0):
    return tgt.at[idx].add(src)

def _segment_sum(src, seg, n):
    return jax.ops.segment_sum(src, seg, n)
kernel_name = 'mk_adj_seq_d1_adj_r2_38fae8'

def setup_inputs(seed: int=0):
    np.random.seed(seed)
    _w = jnp.asarray

    def _rec_inputs():
        import jax
        import jax.numpy as jnp
        _gk = jax.random.key(seed)
        x = -0.0002928 + 1 * jax.random.normal(jax.random.fold_in(_gk, 1), (64, 128, 256), jnp.float32)
        _a = jax.random.bernoulli(jax.random.fold_in(_gk, 2), 0.03125, (64, 128, 128))
        _af = _a.astype(jnp.float32)
        adj = _af
        return (x, adj)
    x, adj = _rec_inputs()

    def _L0_gnn_setup():
        import jax, jax.numpy as jnp
        import numpy as np
        import math
        D_MODEL = 256
        NHEAD = 8
        HEAD_DIM = D_MODEL // NHEAD
        LN_EPS = 1e-05

        def _layernorm(x, g, b):
            mu = jnp.mean(x, axis=-1, keepdims=True)
            var = jnp.mean(jnp.square(x - mu), axis=-1, keepdims=True)
            return (x - mu) * jax.lax.rsqrt(var + LN_EPS) * g + b
        key = jax.random.key(seed)
        ks = jax.random.split(key, 12)
        B, N, D = (4, 1024, D_MODEL)
        s = 1.0 / math.sqrt(D)
        inp = {'hidden': jax.random.normal(ks[0], (B, N, D), jnp.float32), 'adjacency': (jax.random.uniform(ks[1], (B, N, N)) > 0.98).astype(jnp.float32), 'Wq': jax.random.normal(ks[2], (D, D), jnp.float32) * s, 'bq': jnp.zeros((D,), jnp.float32), 'Wk': jax.random.normal(ks[3], (D, D), jnp.float32) * s, 'bk': jnp.zeros((D,), jnp.float32), 'Wv': jax.random.normal(ks[4], (D, D), jnp.float32) * s, 'bv': jnp.zeros((D,), jnp.float32), 'Wo': jax.random.normal(ks[5], (D, D), jnp.float32) * s, 'bo': jnp.zeros((D,), jnp.float32), 'g1': jnp.ones((D,), jnp.float32), 'b1': jnp.zeros((D,), jnp.float32), 'g2': jnp.ones((D,), jnp.float32), 'b2': jnp.zeros((D,), jnp.float32), 'Wf1': jax.random.normal(ks[6], (D, 4 * D), jnp.float32) * s, 'bf1': jnp.zeros((4 * D,), jnp.float32), 'Wf2': jax.random.normal(ks[7], (4 * D, D), jnp.float32) * (1.0 / math.sqrt(4 * D)), 'bf2': jnp.zeros((D,), jnp.float32)}
        return inp
    _L0_gnn_all = _L0_gnn_setup()
    _L0_gnn_in = {k: v for k, v in _L0_gnn_all.items() if k in ('Wq', 'bq', 'Wk', 'bk', 'Wv', 'bv', 'Wo', 'bo', 'g1', 'b1', 'g2', 'b2', 'Wf1', 'bf1', 'Wf2', 'bf2')}
    del _L0_gnn_all
    return {'x': x, 'adj': adj, 'L0_gnn_Wq': _L0_gnn_in['Wq'], 'L0_gnn_bq': _L0_gnn_in['bq'], 'L0_gnn_Wk': _L0_gnn_in['Wk'], 'L0_gnn_bk': _L0_gnn_in['bk'], 'L0_gnn_Wv': _L0_gnn_in['Wv'], 'L0_gnn_bv': _L0_gnn_in['bv'], 'L0_gnn_Wo': _L0_gnn_in['Wo'], 'L0_gnn_bo': _L0_gnn_in['bo'], 'L0_gnn_g1': _L0_gnn_in['g1'], 'L0_gnn_b1': _L0_gnn_in['b1'], 'L0_gnn_g2': _L0_gnn_in['g2'], 'L0_gnn_b2': _L0_gnn_in['b2'], 'L0_gnn_Wf1': _L0_gnn_in['Wf1'], 'L0_gnn_bf1': _L0_gnn_in['bf1'], 'L0_gnn_Wf2': _L0_gnn_in['Wf2'], 'L0_gnn_bf2': _L0_gnn_in['bf2']}

def reference(x, adj, L0_gnn_Wq, L0_gnn_bq, L0_gnn_Wk, L0_gnn_bk, L0_gnn_Wv, L0_gnn_bv, L0_gnn_Wo, L0_gnn_bo, L0_gnn_g1, L0_gnn_b1, L0_gnn_g2, L0_gnn_b2, L0_gnn_Wf1, L0_gnn_bf1, L0_gnn_Wf2, L0_gnn_bf2):
    import jax
    import jax.numpy as jnp

    def _L0_gnn_ref(hidden, adjacency, Wq, bq, Wk, bk, Wv, bv, Wo, bo, g1, b1, g2, b2, Wf1, bf1, Wf2, bf2):
        import jax, jax.numpy as jnp
        import numpy as np
        import math
        D_MODEL = 256
        NHEAD = 8
        HEAD_DIM = D_MODEL // NHEAD
        LN_EPS = 1e-05

        def _layernorm(x, g, b):
            mu = jnp.mean(x, axis=-1, keepdims=True)
            var = jnp.mean(jnp.square(x - mu), axis=-1, keepdims=True)
            return (x - mu) * jax.lax.rsqrt(var + LN_EPS) * g + b
        B, N, D = hidden.shape
        H, Hd = (NHEAD, HEAD_DIM)
        normed = _layernorm(hidden, g1, b1)
        q = (normed @ Wq + bq).reshape(B, N, H, Hd).transpose(0, 2, 1, 3)
        k = (normed @ Wk + bk).reshape(B, N, H, Hd).transpose(0, 2, 1, 3)
        v = (normed @ Wv + bv).reshape(B, N, H, Hd).transpose(0, 2, 1, 3)
        logits = jnp.einsum('bhnd,bhmd->bhnm', q, k) / math.sqrt(Hd)
        adj = adjacency[:, None, :, :]
        logits = logits + (2.0 * adj - 1.0)
        weights = jax.nn.softmax(logits, axis=-1)
        weights = weights * (0.25 + 0.75 * adj)
        weights = weights / jnp.maximum(weights.sum(axis=-1, keepdims=True), 1e-06)
        attended = jnp.einsum('bhnm,bhmd->bhnd', weights, v)
        attended = attended.transpose(0, 2, 1, 3).reshape(B, N, D)
        hidden = hidden + attended @ Wo + bo
        h2 = _layernorm(hidden, g2, b2)
        ff = jax.nn.gelu(h2 @ Wf1 + bf1, approximate=False) @ Wf2 + bf2
        return hidden + ff
    x = _L0_gnn_ref(x, adj, L0_gnn_Wq, L0_gnn_bq, L0_gnn_Wk, L0_gnn_bk, L0_gnn_Wv, L0_gnn_bv, L0_gnn_Wo, L0_gnn_bo, L0_gnn_g1, L0_gnn_b1, L0_gnn_g2, L0_gnn_b2, L0_gnn_Wf1, L0_gnn_bf1, L0_gnn_Wf2, L0_gnn_bf2)
    return x

_drawn_inputs = setup_inputs


def setup_inputs(seed=0):
    import zlib

    import numpy as np

    out = dict(_drawn_inputs(seed))
    spreads = {'L0_gnn_bq': (0.0, 0.322),
     'L0_gnn_bk': (0.0, 0.8),
     'L0_gnn_bv': (0.0, 0.1),
     'L0_gnn_bo': (0.0, 0.1),
     'L0_gnn_g1': (1.0, 0.2),
     'L0_gnn_b1': (0.0, 0.1),
     'L0_gnn_g2': (1.0, 0.2),
     'L0_gnn_b2': (0.0, 0.1),
     'L0_gnn_bf1': (0.0, 0.1),
     'L0_gnn_bf2': (0.0, 0.1)}
    factors = {}
    for name, (base, spread) in spreads.items():
        noise = np.random.default_rng([zlib.crc32(name.encode()), seed]).standard_normal(out[name].shape)
        drawn = base * np.exp(spread * noise) if base else spread * noise
        out[name] = jnp.asarray(drawn.astype(out[name].dtype))
    for name, factor in factors.items():
        out[name] = (out[name] * factor).astype(out[name].dtype)
    return out
```

```python
from contextlib import ExitStack

import concourse.bass as bass
from concourse import mybir

F32 = mybir.dt.float32
F16 = mybir.dt.float16
BF16 = mybir.dt.bfloat16
ACT = mybir.ActivationFunctionType
ALU = mybir.AluOpType
AX = mybir.AxisListType


def gnn_layer(nc, x, adj, Wq, bq, Wk, bk, Wv, bv, Wo, bo, g1, b1, g2, b2, Wf1, bf1, Wf2, bf2, out):
    B, N, D = x.shape
    FF = Wf1.shape[1]
    H = 8
    HD = D // H
    P = 128
    DC = D // P
    FC = FF // P
    U = 4
    UNITS = B // U
    T = U * N
    HC = P // HD
    VW = HD + 2
    WS = 16.0
    LN_EPS = 1e-5
    GUARD = 1e-6
    EXP_SCALE = float(HD) ** -0.5 / (WS * WS)
    assert N == P and T == 512 and UNITS % 2 == 0

    ctx = ExitStack()
    with ctx:
        def sb(name, shape, dt=F32):
            return ctx.enter_context(nc.sbuf_tensor(name, shape, dt))

        def bank(name):
            return ctx.enter_context(nc.psum_tensor(name, [P, 512], F32))

        def sem(name):
            return ctx.enter_context(nc.semaphore(name))

        hid = sb("hid", [P, B, D])
        w_qkvo = {n: (sb(f"w{n}_hi", [P, DC, D], F16), sb(f"w{n}_lo", [P, DC, D], F16)) for n in "qkvo"}
        wf1_hi, wf1_lo = sb("wf1_hi", [P, DC, FF], F16), sb("wf1_lo", [P, DC, FF], F16)
        wf2_hi, wf2_lo = sb("wf2_hi", [P, FC, D], F16), sb("wf2_lo", [P, FC, D], F16)
        ln_cols = sb("ln_cols", [P, 4, DC])
        bias_cols = sb("bias_cols", [P, 4 + FC])
        bias_folded = sb("bias_folded", [P, 4 + FC])
        bv_row, bo_row, bf2_row = sb("bv_row", [P, D]), sb("bo_row", [P, D]), sb("bf2_row", [P, D])
        bv_parts = sb("bv_parts", [P, D], F16)
        bv_pick = sb("bv_pick", [P, P], F16)
        ident = sb("ident", [P, P])
        ident_bf = sb("ident_bf", [P, P], BF16)
        ones_col = sb("ones_col", [P, 2], F16)
        minus_one = sb("minus_one", [P, 1])
        minus_half = sb("minus_half", [P, U])
        eps = sb("eps", [P, U])
        nrm = sb("nrm", [P, U, D])
        bn = sb("bn", [P, U, 6])
        mv = sb("mv", [P, U, 2])
        var_eps = sb("var_eps", [P, U])
        rstd = sb("rstd", [P, U])
        nT_hi, nT_lo = sb("nT_hi", [P, DC, T], F16), sb("nT_lo", [P, DC, T], F16)
        adj_sb = sb("adj_sb", [P, U, P])
        expo = [sb(f"expo{p}", [P, U, P]) for p in range(2)]
        weight = [sb(f"weight{p}", [P, U, P]) for p in range(2)]
        mix = sb("mix", [P, U, P])
        qT = sb("qT", [P, 2, DC, T], F16)
        spread = sb("spread", [P, 2, HC, 2, DC, T], F16)
        kT = [(sb(f"kT_hi{p}", [P, DC, T], F16), sb(f"kT_lo{p}", [P, DC, T], F16)) for p in range(2)]
        v = [(sb(f"v_hi{p}", [P, U, H, VW], F16), sb(f"v_lo{p}", [P, U, H, VW], F16)) for p in range(2)]
        shift = sb("shift", [P, H], BF16)
        W1 = H * P
        scratch = sb("scratch", [P, 7 * W1])
        e32 = [scratch[:, p * W1:(p + 1) * W1] for p in range(2)]
        p32 = [scratch[:, (2 + p) * W1:(3 + p) * W1] for p in range(2)]
        halves = scratch[:, 4 * W1:7 * W1].bitcast(F16)
        p_hi = [halves[:, p * W1:(p + 1) * W1] for p in range(2)]
        p_lo = [halves[:, (2 + p) * W1:(3 + p) * W1] for p in range(2)]
        e_gate = [halves[:, (4 + p) * W1:(5 + p) * W1] for p in range(2)]
        raw = scratch[:, 0:4 * DC * D].rearrange("p (w c n) -> p w c n", w=4, c=DC)
        raw_f1 = scratch[:, 4 * DC * D:4 * DC * D + DC * FF].rearrange("p (c n) -> p c n", c=DC)
        raw_f2 = scratch[:, 4 * DC * D + DC * FF:4 * DC * D + DC * FF + FC * D].rearrange(
            "p (c n) -> p c n", c=FC)
        s1_small, denom, recip = sb("s1_small", [P, H]), sb("denom", [P, H]), sb("recip", [P, H])
        att = sb("att", [P, U, D])
        aT_hi, aT_lo = sb("aT_hi", [P, DC, 2 * N], F16), sb("aT_lo", [P, DC, 2 * N], F16)
        flat = spread[:, :, :, :, :, :].rearrange("p a r l c t -> p (a r l c t)")
        h32 = flat[:, 0:2 * 4 * T].bitcast(F32).rearrange("p (f t) -> p f t", t=T)
        h_hi = flat[:, 8 * T:(8 + FC) * T].rearrange("p (f t) -> p f t", t=T)
        h_lo = flat[:, (8 + FC) * T:(8 + 2 * FC) * T].rearrange("p (f t) -> p f t", t=T)

        front = [bank("front0"), bank("front1")]
        rough = ctx.enter_context(nc.psum_tensor("rough", [P, 1024], F32))
        logit = ctx.enter_context(nc.psum_tensor("logit", [P, 1024], F32))
        mixed = bank("mixed")
        back = bank("back")
        hbank = [rough[:, 0:512], rough[:, 512:1024], logit[:, 0:512], logit[:, 512:1024]]
        obank = [mixed, back]

        x_loaded = sem("x_loaded")
        adj_loaded = sem("adj_loaded")
        w_loaded = [sem(f"w_loaded{n}") for n in range(2)]
        small_loaded = sem("small_loaded")
        ident_set = sem("ident_set")
        consts_set = sem("consts_set")
        bias_made = sem("bias_made")
        scaled = sem("scaled")
        w_hi_made = sem("w_hi_made")
        w_made = sem("w_made")
        bias_ready = sem("bias_ready")
        stats_done = sem("stats_done")
        moments = sem("moments")
        eps_added = sem("eps_added")
        rstd_ready = sem("rstd_ready")
        normed = sem("normed")
        bias_added = sem("bias_added")
        norm_T = sem("norm_T")
        norm_T_hi = sem("norm_T_hi")
        norm_T_lo = sem("norm_T_lo")
        adj_T = sem("adj_T")
        expo_ready = sem("expo_ready")
        mix_ready = sem("mix_ready")
        weight_ready = sem("weight_ready")
        qk = sem("qk")
        qk_hi = sem("qk_hi")
        qk_lo = sem("qk_lo")
        val = sem("val")
        val_hi = sem("val_hi")
        val_lo = sem("val_lo")
        q_spread = sem("q_spread")
        rough_done = sem("rough_done")
        shift_ready = sem("shift_ready")
        logit_done = sem("logit_done")
        exp_ready = sem("exp_ready")
        p_ready = sem("p_ready")
        p_hi_ready = sem("p_hi_ready")
        p_lo_ready = sem("p_lo_ready")
        gate_ready = sem("gate_ready")
        mixed_done = sem("mixed_done")
        s1_scaled = sem("s1_scaled")
        denom_ready = sem("denom_ready")
        recip_ready = sem("recip_ready")
        att_ready = sem("att_ready")
        att_T = sem("att_T")
        att_T_hi = sem("att_T_hi")
        att_T_lo = sem("att_T_lo")
        proj_done = sem("proj_done")
        resid_done = sem("resid_done")
        ff1_done = sem("ff1_done")
        gelu_done = sem("gelu_done")
        h_hi_ready = sem("h_hi_ready")
        h_lo_ready = sem("h_lo_ready")
        ff2_done = sem("ff2_done")
        out_ready = sem("out_ready")
        stored = sem("stored")

        block = ctx.enter_context(nc.Block())

        def graph(ap4, j):
            return ap4[:, j, :].unsqueeze(1).to_broadcast([P, H, P])

        @block.sync
        def _(sp):
            def load_x(u):
                sp.dma_start(hid[:, bass.ds(u * U, U), :],
                             x[bass.ds(u * U, U), :, :].rearrange("b p n -> p b n")).then_inc(x_loaded, 16)

            def load_adj(u):
                sp.dma_start(adj_sb[:, :, :],
                             adj[bass.ds(u * U, U), :, :].rearrange("b p n -> p b n")).then_inc(adj_loaded, 16)

            def spread_q(u, par):
                sp.wait_ge(qk_lo, u * 4 + 2)
                for r in range(HC):
                    rows = slice(r * HD, (r + 1) * HD)
                    sp.dma_start(spread[rows, par, r, :, :, :], qT[rows, :, :, :]).then_inc(q_spread, 16)

            load_x(0)
            sp.dma_start(ln_cols[:, 0, :], g1.rearrange("(c p) -> p c", p=P),
                         allow_slow_non_contiguous=True).then_inc(small_loaded, 16)
            sp.dma_start(ln_cols[:, 1, :], b1.rearrange("(c p) -> p c", p=P),
                         allow_slow_non_contiguous=True).then_inc(small_loaded, 16)
            sp.dma_start(ln_cols[:, 2, :], g2.rearrange("(c p) -> p c", p=P),
                         allow_slow_non_contiguous=True).then_inc(small_loaded, 16)
            sp.dma_start(ln_cols[:, 3, :], b2.rearrange("(c p) -> p c", p=P),
                         allow_slow_non_contiguous=True).then_inc(small_loaded, 16)
            sp.dma_start(bias_cols[:, 0:2], bq.rearrange("(c p) -> p c", p=P),
                         allow_slow_non_contiguous=True).then_inc(small_loaded, 16)
            sp.dma_start(bias_cols[:, 2:4], bk.rearrange("(c p) -> p c", p=P),
                         allow_slow_non_contiguous=True).then_inc(small_loaded, 16)
            sp.dma_start(bias_cols[:, 4:4 + FC], bf1.rearrange("(c p) -> p c", p=P),
                         allow_slow_non_contiguous=True).then_inc(small_loaded, 16)
            for row, b in ((bv_row, bv), (bo_row, bo), (bf2_row, bf2)):
                sp.dma_start(row[:, :], b.rearrange("(a n) -> a n", a=1).to_broadcast([P, D])).then_inc(small_loaded, 16)
            load_adj(0)
            sp.wait_ge(x_loaded, 16)
            load_x(1)
            sp.wait_ge(consts_set, 2)
            spread_q(0, 0)
            sp.wait_ge(x_loaded, 32)
            load_x(2)
            sp.wait_ge(adj_T, 1)
            load_adj(1)

            def unit(u, par, load=True, nxt=True):
                if load:
                    sp.wait_ge(x_loaded, u * 16 + 48)
                    load_x(u + 3)
                if nxt:
                    spread_q(u + 1, 1 - par)
                    sp.wait_ge(adj_T, u + 2)

            unit(0, 0)
            load_adj(2)
            with sp.Fori(0, UNITS // 2 - 2) as i:
                u = i * 2 + 1
                unit(u, 1)
                load_adj(u + 2)
                unit(u + 1, 0)
                load_adj(u + 3)
            unit(UNITS - 3, 1, load=False)
            load_adj(UNITS - 1)
            unit(UNITS - 2, 0, load=False)

            def store(w, n):
                sp.wait_ge(out_ready, n + 1)
                sp.dma_start(out[bass.ds(w, 2), :, :].rearrange("b p n -> p b n"),
                             hid[:, bass.ds(w, 2), :]).then_inc(stored, 16)

            with sp.Fori(0, B // 2) as n:
                store(n * 2, n)
            sp.wait_ge(stored, 16 * (B // 2))

        @block.gpsimd
        def _(pool):
            pool.memset(ident[:, :], 0.0).then_inc(ident_set, 1)
            pool.wait_ge(ident_set, 1)
            pool.affine_select(out=ident[:, :], in_=ident[:, :], compare_op=ALU.not_equal, fill=1.0,
                               base=0, pattern=[[-1, P]], channel_multiplier=1).then_inc(ident_set, 1)
            pool.memset(minus_half[:, :], -0.5)
            pool.memset(eps[:, :], LN_EPS)
            pool.memset(bv_pick[:, :], 0.0).then_inc(consts_set, 1)
            pool.memset(spread[:, :, :, :, :, :].rearrange("p a r l c t -> p (a r l c t)").bitcast(F32), 0.0)\
                .then_inc(consts_set, 1)

            def inv_std(n):
                pool.wait_ge(moments, n * 2 + 2)
                if not (isinstance(n, int) and n == 0):
                    pool.wait_ge(normed, n)
                pool.tensor_tensor(var_eps[:, :], mv[:, :, 1], eps[:, :], ALU.add)\
                    .then_inc(eps_added, 1)
                pool.wait_ge(eps_added, n + 1)
                pool.tensor_tensor(rstd[:, :], var_eps[:, :], minus_half[:, :], ALU.pow).then_inc(rstd_ready, 1)

            def add_bias(u, n, row):
                pool.wait_ge(normed, n + 1)
                h = hid[:, bass.ds(u * U, U), :]
                pool.tensor_tensor(h, h, row[:, :].unsqueeze(1).to_broadcast([P, U, D]), ALU.add)\
                    .then_inc(bias_added, 1)

            def gated(u, j, par):
                b = u * U + j
                pool.wait_ge(exp_ready, b + 1)
                if j == 0:
                    pool.wait_ge(expo_ready, u + 1)
                if not (isinstance(b, int) and b < 2):
                    pool.wait_ge(mixed_done, b - 1)
                pool.tensor_tensor(e_gate[j % 2].rearrange("p (h q) -> p h q", q=P),
                                   e32[j % 2].rearrange("p (h q) -> p h q", q=P),
                                   graph(expo[par], j), ALU.mult).then_inc(gate_ready, 1)

            pool.wait_ge(small_loaded, 160)
            inv_std(0)
            add_bias(0, 0, bo_row)
            inv_std(1)
            add_bias(1, 1, bo_row)

            def unit(u, par, ahead=True):
                for j in range(U):
                    gated(u, j, par)
                    if j == 1 and ahead:
                        inv_std(u + 2)
                if ahead:
                    add_bias(u + 2, u + 2, bo_row)

            unit(0, 0)
            with pool.Fori(0, UNITS // 2 - 2) as i:
                u = i * 2 + 1
                unit(u, 1)
                unit(u + 1, 0)
            unit(UNITS - 3, 1)
            unit(UNITS - 2, 0, ahead=False)
            unit(UNITS - 1, 1, ahead=False)

            with pool.Fori(0, UNITS) as w:
                inv_std(w + UNITS)
                add_bias(w, w + UNITS, bf2_row)

        @block.scalar
        def _(act):
            for n, (dst, src) in enumerate(((raw[:, 0, :, :], Wq), (raw[:, 1, :, :], Wk), (raw[:, 2, :, :], Wv),
                                            (raw[:, 3, :, :], Wo), (raw_f1, Wf1), (raw_f2, Wf2))):
                act.dma_start(dst, src.rearrange("(c p) n -> p c n", p=P)).then_inc(w_loaded[n // 4], 16)

            def norm_hi(n, c):
                act.wait_ge(norm_T, n * 2 + c + 1)
                act.activation(nT_hi[:, c, :], front[c][:, :], ACT.Copy).then_inc(norm_T_hi, 1)

            def expo_of(u, par):
                if not (isinstance(u, int) and u < 2):
                    act.wait_ge(gate_ready, u * U - U)
                act.wait_ge(adj_T, u + 1)
                act.activation(expo[par][:, :, :].rearrange("p b q -> p (b q)"), front[0][:, :], ACT.Exp,
                               bias=minus_one[:, :], scale=2.0).then_inc(expo_ready, 1)

            def qk_part(u, par, m):
                if m == 0 and not (isinstance(u, int) and u == 0):
                    act.wait_ge(q_spread, u * 64)
                act.wait_ge(qk, u * 4 + m + 1)
                dst = qT[:, 0, m, :] if m < 2 else kT[par][0][:, m - 2, :]
                act.activation(dst, front[1 - m % 2][:, :], ACT.Identity,
                               bias=bias_folded[:, m:m + 1]).then_inc(qk_hi, 1)

            def val_part(u, par, m):
                act.wait_ge(val, u * 2 + m + 1)
                act.activation(v[par][0][:, 2 * m:2 * m + 2, :, 0:HD].rearrange("p b h d -> p (b h) d"),
                               front[1 - m][:, :].rearrange("p (g d) -> p g d", d=HD),
                               ACT.Copy).then_inc(val_hi, 1)

            def piece(u, par, k):
                if k == 0:
                    norm_hi(u, 0)
                    norm_hi(u, 1)
                elif k == 1:
                    expo_of(u, par)
                elif k < 6:
                    qk_part(u, par, k - 2)
                else:
                    val_part(u, par, k - 6)

            def part_of_p(b, s):
                act.wait_ge(p_ready, b + 1)
                if not (isinstance(b, int) and b < 2):
                    act.wait_ge(mixed_done, b - 1)
                act.activation(p_hi[s], p32[s], ACT.Copy).then_inc(p_hi_ready, 1)

            def att_part(p):
                act.wait_ge(att_T, p + 1)
                act.activation(aT_hi[:, :, :].rearrange("p c t -> p (c t)"), back[:, :], ACT.Copy)\
                    .then_inc(att_T_hi, 1)

            def exponent(b, s):
                act.wait_ge(logit_done, b + 1)
                if not (isinstance(b, int) and b < 2):
                    act.wait_ge(p_ready, b - 1)
                    act.wait_ge(gate_ready, b - 1)
                act.activation(e32[s], logit[:, :], ACT.Exp, scale=EXP_SCALE).then_inc(exp_ready, 1)

            act.wait_ge(bias_ready, 1)
            for k in range(8):
                piece(0, 0, k)

            def unit(u, par, first=False, nxt=True):
                for j in range(U):
                    b = u * U + j
                    if not (first and j == 0):
                        part_of_p(b - 1, (j - 1) % 2)
                    if nxt:
                        piece(u + 1, 1 - par, 2 * j)
                    if j == 1 and not first:
                        att_part(u * 2 - 1)
                    if j == 3:
                        att_part(u * 2)
                    exponent(b, j % 2)
                    if nxt:
                        piece(u + 1, 1 - par, 2 * j + 1)

            unit(0, 0, first=True)
            with act.Fori(0, UNITS // 2 - 2) as i:
                u = i * 2 + 1
                unit(u, 1)
                unit(u + 1, 0)
            unit(UNITS - 3, 1)
            unit(UNITS - 2, 0)
            unit(UNITS - 1, 1, nxt=False)
            part_of_p(B - 1, 1)
            att_part(B // 2 - 1)

            def gelu(w, f):
                act.wait_ge(ff1_done, w * FC + f + 1)
                if f >= 4 or not (isinstance(w, int) and w == 0):
                    act.wait_ge(h_lo_ready, w * FC + f - 3)
                act.activation(h32[:, f % 4, :], hbank[f % 4], ACT.Gelu,
                               bias=bias_folded[:, 4 + f:5 + f], scale=1.0 / WS).then_inc(gelu_done, 1)

            def ff_unit(w, nxt=True):
                for f in range(FC):
                    gelu(w, f)
                if nxt:
                    norm_hi(w + UNITS + 1, 0)
                    norm_hi(w + UNITS + 1, 1)

            norm_hi(UNITS, 0)
            norm_hi(UNITS, 1)
            ff_unit(0)
            with act.Fori(1, UNITS - 1) as w:
                ff_unit(w)
            ff_unit(UNITS - 1, nxt=False)

        @block.tensor
        def _(pe):
            pe.wait_ge(small_loaded, 160)
            pe.wait_ge(w_loaded[0], 64)
            for w in range(2):
                for c in range(DC):
                    for k in range(DC):
                        pe.matmul(mixed[:, 2 * w + c:2 * w + c + 1], raw[:, w, k, c * P:(c + 1) * P],
                                  ln_cols[:, 1, k:k + 1], start=(k == 0), stop=(k == DC - 1))
            for k in range(DC):
                pe.matmul(back[:, 0:D], ln_cols[:, 1, k:k + 1].to_broadcast([P, P]), raw[:, 2, k, :],
                          start=(k == 0), stop=(k == DC - 1))
            pe.wait_ge(w_loaded[1], 32)
            for f in range(FC):
                for k in range(DC):
                    mm = pe.matmul(mixed[:, 4 + f:5 + f], raw_f1[:, k, f * P:(f + 1) * P],
                                   ln_cols[:, 3, k:k + 1], start=(k == 0), stop=(k == DC - 1))
            mm.then_inc(bias_made, 1)
            pe.wait_ge(ident_set, 2)

            def products(parts):
                return [(l, r) for lh, ll, rh, rl in parts for l, r in ((lh, rh), (lh, rl), (ll, rh))]

            def accumulate(dst, pairs):
                for n, (lhs, rhs) in enumerate(pairs):
                    mm = pe.matmul(dst, lhs, rhs, start=(n == 0), stop=(n == len(pairs) - 1))
                return mm

            def norm_transposes(n, c):
                if c == 0:
                    pe.wait_ge(normed, n + 1)
                for j in range(U):
                    mm = pe.transpose(front[c][:, j * P:(j + 1) * P], nrm[:, j, c * P:(c + 1) * P], ident[:, :])
                mm.then_inc(norm_T, 1)

            def piece(u, par, k):
                if k == 0:
                    for c in range(DC):
                        if not (isinstance(u, int) and u == 0):
                            pe.wait_ge(val_lo, u * 2 - c)
                        norm_transposes(u, c)
                elif k == 1:
                    pe.wait_ge(norm_T_lo, u * 2 + 1)
                    pe.wait_ge(adj_loaded, u * 16 + 16)
                    for j in range(U):
                        mm = pe.transpose(front[0][:, j * P:(j + 1) * P], adj_sb[:, j, :], ident[:, :])
                    mm.then_inc(adj_T, 1)
                elif k < 6:
                    m = k - 2
                    if m == 0:
                        pe.wait_ge(norm_T_lo, u * 2 + 2)
                    elif m == 1:
                        pe.wait_ge(weight_ready, u + 1)
                    else:
                        pe.wait_ge(qk_lo, u * 4 + m - 1)
                    w_hi, w_lo = w_qkvo["qk"[m // 2]]
                    cols = slice((m % 2) * P, (m % 2 + 1) * P)
                    accumulate(front[1 - m % 2][:, :],
                               products([(w_hi[:, c, cols], w_lo[:, c, cols], nT_hi[:, c, :], nT_lo[:, c, :])
                                         for c in range(DC)])).then_inc(qk, 1)
                else:
                    m = k - 6
                    pe.wait_ge(qk_lo, u * 4 + 3 + m)
                    w_hi, w_lo = w_qkvo["v"]
                    for jj in range(2):
                        tok = slice((2 * m + jj) * P, (2 * m + jj + 1) * P)
                        mm = accumulate(front[1 - m][:, jj * D:(jj + 1) * D],
                                        products([(nT_hi[:, c, tok], nT_lo[:, c, tok], w_hi[:, c, :], w_lo[:, c, :])
                                                  for c in range(DC)]) + [(bv_pick[:, :], bv_parts[:, :])])
                    mm.then_inc(val, 1)

            def rough_logits(u, j, par):
                b = u * U + j
                if j == 0:
                    pe.wait_ge(q_spread, u * 64 + 64)
                    pe.wait_ge(qk_lo, u * 4 + 4)
                if not (isinstance(b, int) and b == 0):
                    pe.wait_ge(shift_ready, b)
                tok = slice(j * P, (j + 1) * P)
                for h in range(H):
                    c, r = divmod(h, HC)
                    mm = pe.matmul(rough[:, h * P:(h + 1) * P], spread[:, par, r, 0, c, tok],
                                   kT[par][0][:, c, tok], start=True, stop=True)
                mm.then_inc(rough_done, 1)

            def logits(u, j, par):
                b = u * U + j
                if not (isinstance(b, int) and b == 0):
                    pe.wait_ge(exp_ready, b)
                tok = slice(j * P, (j + 1) * P)
                for c in range(DC):
                    k_hi, k_lo = kT[par][0][:, c, tok], kT[par][1][:, c, tok]
                    q_hi, q_lo = spread[:, par, :, 0, c, tok], spread[:, par, :, 1, c, tok]
                    for n, (lhs, rhs) in enumerate(((k_hi, q_hi), (k_hi, q_lo), (k_lo, q_hi))):
                        pe.matmul(logit[:, c * HC * P:(c + 1) * HC * P].rearrange("p (r q) -> p r q", q=P),
                                  lhs, rhs, start=(n == 0), stop=False)
                pe.wait_ge(shift_ready, b + 1)
                for h in range(H):
                    mm = pe.matmul(logit[:, h * P:(h + 1) * P], shift[:, h:h + 1].to_broadcast([P, P]),
                                   ident_bf[:, :], start=False, stop=(h % HC == HC - 1))
                mm.then_inc(logit_done, 1)

            def mix_values(b, j, par, check_v):
                pe.wait_ge(p_lo_ready, b + 1)
                if check_v is not None:
                    pe.wait_ge(val_lo, check_v)
                if not (isinstance(b, int) and b == 0):
                    pe.wait_ge(att_ready, b)
                s = j % 2
                v_hi, v_lo = v[par]
                for h in range(H):
                    cols = slice(h * P, (h + 1) * P)
                    accumulate(mixed[:, h * VW:h * VW + HD + 1],
                               [(p_hi[s][:, cols], v_hi[:, j, h, 0:HD + 1]), (p_hi[s][:, cols], v_lo[:, j, h, 0:HD + 1]),
                                (p_lo[s][:, cols], v_hi[:, j, h, 0:HD + 1])])
                pe.wait_ge(gate_ready, b + 1)
                for h in range(H):
                    mm = pe.matmul(mixed[:, H * VW + h:H * VW + h + 1], e_gate[s][:, h * P:(h + 1) * P],
                                   ones_col[:, 0:1], start=True, stop=True)
                mm.then_inc(mixed_done, 1)

            def att_transposes(p, s):
                pe.wait_ge(att_ready, p * 2 + 2)
                if not (isinstance(p, int) and p == 0):
                    pe.wait_ge(resid_done, p)
                for c in range(DC):
                    for jj in range(2):
                        mm = pe.transpose(back[:, (c * 2 + jj) * P:(c * 2 + jj + 1) * P],
                                          att[:, s + jj, c * P:(c + 1) * P], ident[:, :])
                mm.then_inc(att_T, 1)

            def project(p):
                pe.wait_ge(att_T_lo, p + 1)
                w_hi, w_lo = w_qkvo["o"]
                for jj in range(2):
                    tok = slice(jj * P, (jj + 1) * P)
                    mm = accumulate(back[:, jj * D:(jj + 1) * D],
                                    products([(aT_hi[:, c, tok], aT_lo[:, c, tok], w_hi[:, c, :], w_lo[:, c, :])
                                              for c in range(DC)]))
                mm.then_inc(proj_done, 1)

            piece(0, 0, 0)
            piece(0, 0, 1)
            pe.wait_ge(w_made, 4)
            pe.wait_ge(bias_ready, 1)
            for k in range(2, 8):
                piece(0, 0, k)

            def unit(u, par, first=False, nxt=True):
                for j in range(U):
                    b = u * U + j
                    rough_logits(u, j, par)
                    if nxt:
                        piece(u + 1, 1 - par, 2 * j)
                    if j == 0 and not first:
                        project(u * 2 - 2)
                    if j == 1 and not first:
                        att_transposes(u * 2 - 1, 2)
                    if j == 2 and not first:
                        project(u * 2 - 1)
                    if j == 3:
                        att_transposes(u * 2, 0)
                    logits(u, j, par)
                    if nxt:
                        piece(u + 1, 1 - par, 2 * j + 1)
                    if j > 0:
                        mix_values(b - 1, j - 1, par, u * 2 + 2 if j == 1 else None)
                    elif not first:
                        mix_values(b - 1, U - 1, 1 - par, None)

            unit(0, 0, first=True)
            with pe.Fori(0, UNITS // 2 - 2) as i:
                u = i * 2 + 1
                unit(u, 1)
                unit(u + 1, 0)
            unit(UNITS - 3, 1)
            unit(UNITS - 2, 0)
            unit(UNITS - 1, 1, nxt=False)
            project(B // 2 - 2)
            mix_values(B - 1, U - 1, 1, None)
            att_transposes(B // 2 - 1, 2)
            project(B // 2 - 1)

            def ff1(w, f):
                if f >= 4 or not (isinstance(w, int) and w == 0):
                    pe.wait_ge(gelu_done, w * FC + f - 3)
                cols = slice(f * P, (f + 1) * P)
                accumulate(hbank[f % 4],
                           products([(wf1_hi[:, c, cols], wf1_lo[:, c, cols], nT_hi[:, c, :], nT_lo[:, c, :])
                                     for c in range(DC)])).then_inc(ff1_done, 1)

            def ff2(w, m):
                if m == 0 and not (isinstance(w, int) and w == 0):
                    pe.wait_ge(out_ready, w * 2 - 1)
                if m == 1 and not (isinstance(w, int) and w == 0):
                    pe.wait_ge(out_ready, w * 2)
                for jj in range(2):
                    tok = slice((2 * m + jj) * P, (2 * m + jj + 1) * P)
                    for f in range(FC):
                        if m == 0 and jj == 0:
                            pe.wait_ge(h_lo_ready, w * FC + f + 1)
                        for n, (lhs, rhs) in enumerate(products(
                                [(h_hi[:, f, tok], h_lo[:, f, tok], wf2_hi[:, f, :], wf2_lo[:, f, :])])):
                            mm = pe.matmul(obank[m][:, jj * D:(jj + 1) * D], lhs, rhs,
                                           start=(f == 0 and n == 0), stop=(f == FC - 1 and n == 2))
                mm.then_inc(ff2_done, 1)

            def ff_unit(w, nxt=True):
                pe.wait_ge(norm_T_lo, w * 2 + 2 * UNITS + 2)
                for f in range(FC):
                    ff1(w, f)
                if nxt:
                    norm_transposes(w + UNITS + 1, 0)
                    norm_transposes(w + UNITS + 1, 1)
                ff2(w, 0)
                ff2(w, 1)

            norm_transposes(UNITS, 0)
            norm_transposes(UNITS, 1)
            pe.wait_ge(exp_ready, B)
            pe.wait_ge(shift_ready, B)
            pe.wait_ge(resid_done, B // 2)
            ff_unit(0)
            with pe.Fori(1, UNITS - 1) as w:
                ff_unit(w)
            ff_unit(UNITS - 1, nxt=False)

        @block.vector
        def _(dve):
            dve.memset(minus_one[:, :], -1.0)
            dve.memset(ones_col[:, :], 1.0)
            for p in range(2):
                dve.memset(v[p][0][:, :, :, HD:VW], 1.0)
                dve.memset(v[p][1][:, :, :, HD:VW], 0.0)
            dve.wait_ge(ident_set, 2)
            dve.tensor_copy(ident_bf[:, :], ident[:, :])
            dve.wait_ge(consts_set, 1)
            dve.memset(bv_pick[0:1, :], 1.0)
            dve.memset(bv_pick[32:33, :], 1.0)

            def stats(u, n, half):
                for j in (2 * half, 2 * half + 1):
                    ins = dve.bn_stats(bn[:, j, :], hid[:, bass.ds(u * U + j, 1), :].rearrange("p a n -> p (a n)"))
                ins.then_inc(stats_done, 1)

            def aggregate(half):
                for j in (2 * half, 2 * half + 1):
                    ins = dve.bn_aggr(mv[:, j, :], bn[:, j, :])
                ins.then_inc(moments, 1)

            def normalise(u, n, half):
                if half == 0:
                    dve.wait_ge(rstd_ready, n + 1)
                for j in (2 * half, 2 * half + 1):
                    ins = dve.tensor_scalar(nrm[:, j, :], hid[:, bass.ds(u * U + j, 1), :].rearrange("p a n -> p (a n)"),
                                            mv[:, j, 0:1], rstd[:, j:j + 1], ALU.subtract, ALU.mult)
                if half == 1:
                    ins.then_inc(normed, 1)

            dve.wait_ge(x_loaded, 16)
            stats(0, 0, 0)
            dve.wait_ge(stats_done, 1)
            aggregate(0)
            stats(0, 0, 1)
            dve.wait_ge(stats_done, 2)
            aggregate(1)
            normalise(0, 0, 0)
            normalise(0, 0, 1)

            dve.wait_ge(small_loaded, 160)
            dve.wait_ge(bias_made, 1)
            dve.tensor_tensor(bias_folded[:, :], mixed[:, 0:4 + FC], bias_cols[:, :], ALU.add)
            dve.tensor_tensor(bv_row[:, :], back[:, 0:D], bv_row[:, :], ALU.add).then_inc(scaled, 1)
            dve.wait_ge(scaled, 1)
            dve.tensor_scalar(bias_folded[:, 0:4], bias_folded[:, 0:4], WS, None, ALU.mult)
            dve.tensor_scalar(bv_row[:, :], bv_row[:, :], WS, None, ALU.mult).then_inc(scaled, 1)
            dve.wait_ge(scaled, 2)
            dve.tensor_copy(bv_parts[:, :], bv_row[:, :]).then_inc(scaled, 1)
            dve.wait_ge(scaled, 3)
            dve.tensor_tensor(bv_parts[32:64, :], bv_row[32:64, :], bv_parts[32:64, :], ALU.subtract)\
                .then_inc(bias_ready, 1)

            count = 3
            for n, (src, gain, hi, lo) in enumerate((
                    (raw[:, 0, :, :], 0, *w_qkvo["q"]), (raw[:, 1, :, :], 0, *w_qkvo["k"]),
                    (raw[:, 2, :, :], 0, *w_qkvo["v"]), (raw[:, 3, :, :], None, *w_qkvo["o"]),
                    (raw_f1, 2, wf1_hi, wf1_lo), (raw_f2, None, wf2_hi, wf2_lo))):
                if gain is None:
                    ins = dve.tensor_scalar(src, src, WS, None, ALU.mult)
                else:
                    for c in range(DC):
                        ins = dve.tensor_scalar(src[:, c, :], src[:, c, :], ln_cols[:, gain, c:c + 1], WS,
                                                ALU.mult, ALU.mult)
                count += 1
                ins.then_inc(scaled, 1)
                dve.wait_ge(scaled, count)
                dve.tensor_copy(hi[:, :, :], src).then_inc(w_hi_made, 1)
                dve.wait_ge(w_hi_made, n + 1)
                dve.tensor_tensor(lo[:, :, :], src, hi[:, :, :], ALU.subtract).then_inc(w_made, 1)

            def norm_lo(n, c):
                dve.wait_ge(norm_T_hi, n * 2 + c + 1)
                dve.tensor_tensor(nT_lo[:, c, :], front[c][:, :], nT_hi[:, c, :], ALU.subtract)\
                    .then_inc(norm_T_lo, 1)

            def weight_of(u, par):
                dve.wait_ge(expo_ready, u + 1)
                dve.tensor_scalar(mix[:, :, :].rearrange("p b q -> p (b q)"), front[0][:, :], 0.75, 0.25,
                                  ALU.mult, ALU.add).then_inc(mix_ready, 1)
                dve.wait_ge(mix_ready, u + 1)
                dve.tensor_tensor(weight[par][:, :, :], mix[:, :, :], expo[par][:, :, :], ALU.mult)\
                    .then_inc(weight_ready, 1)

            def qk_part(u, par, m):
                dve.wait_ge(qk_hi, u * 4 + m + 1)
                hi = qT[:, 0, m, :] if m < 2 else kT[par][0][:, m - 2, :]
                lo = qT[:, 1, m, :] if m < 2 else kT[par][1][:, m - 2, :]
                dve.scalar_tensor_tensor(lo, front[1 - m % 2][:, :], bias_folded[:, m:m + 1], hi,
                                         ALU.add, ALU.subtract).then_inc(qk_lo, 1)

            def val_part(u, par, m):
                dve.wait_ge(val_hi, u * 2 + m + 1)
                part = [v[par][i][:, 2 * m:2 * m + 2, :, 0:HD].rearrange("p b h d -> p (b h) d") for i in range(2)]
                dve.tensor_tensor(part[1], front[1 - m][:, :].rearrange("p (g d) -> p g d", d=HD), part[0],
                                  ALU.subtract).then_inc(val_lo, 1)

            def piece(u, par, k):
                if k == 0:
                    norm_lo(u, 0)
                    norm_lo(u, 1)
                elif k == 1:
                    weight_of(u, par)
                elif k < 6:
                    qk_part(u, par, k - 2)
                else:
                    val_part(u, par, k - 6)

            def maximum(b):
                dve.wait_ge(rough_done, b + 1)
                if not (isinstance(b, int) and b == 0):
                    dve.wait_ge(logit_done, b)
                dve.tensor_reduce(shift[:, :], rough[:, :].rearrange("p (h k) -> p h k", k=P), AX.X, ALU.max,
                                  negate=True).then_inc(shift_ready, 1)

            def weighted(u, j, par, ahead):
                b = u * U + j
                if ahead and j < 2:
                    dve.wait_ge(stats_done, u * 2 + 5 + j)
                dve.wait_ge(exp_ready, b + 1)
                if not (isinstance(b, int) and b < 2):
                    dve.wait_ge(p_lo_ready, b - 1)
                dve.tensor_tensor(p32[j % 2].rearrange("p (h q) -> p h q", q=P),
                                  e32[j % 2].rearrange("p (h q) -> p h q", q=P),
                                  graph(weight[par], j), ALU.mult).then_inc(p_ready, 1)

            def part_of_p(b, s):
                dve.wait_ge(p_hi_ready, b + 1)
                dve.tensor_tensor(p_lo[s], p32[s], p_hi[s], ALU.subtract).then_inc(p_lo_ready, 1)

            def attended(b, j):
                dve.wait_ge(mixed_done, b + 1)
                dve.tensor_scalar(s1_small[:, :], mixed[:, H * VW:H * VW + H], GUARD, None, ALU.mult)\
                    .then_inc(s1_scaled, 1)
                dve.wait_ge(s1_scaled, b + 1)
                per_head = mixed[:, 0:H * VW].rearrange("p (h d) -> p h d", d=VW)
                dve.tensor_tensor(denom[:, :], per_head[:, :, HD], s1_small[:, :], ALU.max)\
                    .then_inc(denom_ready, 1)
                dve.wait_ge(denom_ready, b + 1)
                dve.reciprocal(recip[:, :], denom[:, :]).then_inc(recip_ready, 1)
                dve.wait_ge(recip_ready, b + 1)
                dve.tensor_tensor(att[:, j, :].rearrange("p (h d) -> p h d", d=HD), per_head[:, :, 0:HD],
                                  recip[:, :].unsqueeze(2).to_broadcast([P, H, HD]), ALU.mult)\
                    .then_inc(att_ready, 1)

            def attended_at(u, j, transposed):
                b = u * U + j
                if transposed is not None and j % 2 == 0:
                    dve.wait_ge(att_T, transposed)
                attended(b, j)

            def att_part(p):
                dve.wait_ge(att_T_hi, p + 1)
                dve.tensor_tensor(aT_lo[:, :, :].rearrange("p c t -> p (c t)"), back[:, :],
                                  aT_hi[:, :, :].rearrange("p c t -> p (c t)"), ALU.subtract).then_inc(att_T_lo, 1)

            def residual(p, b):
                dve.wait_ge(proj_done, p + 1)
                h = hid[:, bass.ds(b, 2), :].rearrange("p a n -> p (a n)")
                dve.scalar_tensor_tensor(h, back[:, :], 1.0 / (WS * WS), h, ALU.mult, ALU.add)\
                    .then_inc(resid_done, 1)

            for k in range(8):
                piece(0, 0, k)
            dve.wait_ge(x_loaded, 32)
            stats(1, 1, 0)
            dve.wait_ge(stats_done, 3)
            aggregate(0)
            stats(1, 1, 1)
            dve.wait_ge(stats_done, 4)
            aggregate(1)
            normalise(1, 1, 0)
            normalise(1, 1, 1)

            def unit(u, par, first=False, nxt=True, ahead=True):
                for j in range(U):
                    b = u * U + j
                    maximum(b)
                    if j >= 2:
                        attended_at(u, j - 2, u * 2 - 1 + j // 2 - 1 if not first else None)
                    elif not first:
                        attended_at(u - 1, j + 2, u * 2 - 1)
                    if not (first and j == 0):
                        part_of_p(b - 1, (j - 1) % 2)
                    if nxt:
                        piece(u + 1, 1 - par, 2 * j)
                    if j == 0 and not first:
                        dve.wait_ge(bias_added, u)
                        residual(u * 2 - 2, u * U - U)
                    if j == 1 and not first:
                        att_part(u * 2 - 1)
                    if j == 2 and not first:
                        residual(u * 2 - 1, u * U - 2)
                    if j == 3:
                        att_part(u * 2)
                    if j == 0 and ahead:
                        dve.wait_ge(x_loaded, u * 16 + 48)
                    if j < 2 and ahead:
                        stats(u + 2, u + 2, j)
                    weighted(u, j, par, ahead)
                    if j < 2 and ahead:
                        aggregate(j)
                    if nxt:
                        piece(u + 1, 1 - par, 2 * j + 1)
                    if j == 2 and ahead:
                        dve.wait_ge(norm_T, u * 2 + 4)
                    if j >= 2 and ahead:
                        normalise(u + 2, u + 2, j - 2)

            unit(0, 0, first=True)
            with dve.Fori(0, UNITS // 2 - 2) as i:
                u = i * 2 + 1
                unit(u, 1)
                unit(u + 1, 0)
            unit(UNITS - 3, 1)
            unit(UNITS - 2, 0, ahead=False)
            unit(UNITS - 1, 1, nxt=False, ahead=False)
            attended_at(UNITS - 1, 2, 2 * UNITS - 2)
            part_of_p(B - 1, 1)
            dve.wait_ge(bias_added, UNITS)
            residual(B // 2 - 2, B - 4)
            attended_at(UNITS - 1, 3, None)
            att_part(B // 2 - 1)
            residual(B // 2 - 1, B - 2)

            def h_parts(w, f, nxt):
                if nxt and f in (2, 4):
                    dve.wait_ge(stats_done, w * 2 + 2 * UNITS + 2 + f // 2)
                dve.wait_ge(gelu_done, w * FC + f + 1)
                if f == 0 and not (isinstance(w, int) and w == 0):
                    dve.wait_ge(ff2_done, w * 2)
                dve.tensor_copy(h_hi[:, f, :], h32[:, f % 4, :]).then_inc(h_hi_ready, 1)
                dve.wait_ge(h_hi_ready, w * FC + f + 1)
                dve.tensor_tensor(h_lo[:, f, :], h32[:, f % 4, :], h_hi[:, f, :], ALU.subtract)\
                    .then_inc(h_lo_ready, 1)

            def finish(w, m):
                dve.wait_ge(ff2_done, w * 2 + m + 1)
                dve.wait_ge(bias_added, w + UNITS + 1)
                h = hid[:, bass.ds(w * U + 2 * m, 2), :].rearrange("p a n -> p (a n)")
                dve.scalar_tensor_tensor(h, obank[m][:, :], 1.0 / WS, h, ALU.mult, ALU.add)\
                    .then_inc(out_ready, 1)

            def ff_unit(w, nxt=True, prev=True):
                for f in range(FC):
                    h_parts(w, f, nxt)
                    if nxt and f in (1, 3):
                        stats(w + 1, w + UNITS + 1, f // 2)
                    if nxt and f in (2, 4):
                        aggregate(f // 2 - 1)
                    if nxt and f in (5, 7):
                        if f == 5:
                            dve.wait_ge(norm_T, w * 2 + 2 * UNITS + 2)
                        normalise(w + 1, w + UNITS + 1, (f - 5) // 2)
                if nxt:
                    norm_lo(w + UNITS + 1, 0)
                    norm_lo(w + UNITS + 1, 1)
                finish(w, 0)
                finish(w, 1)

            dve.wait_ge(resid_done, B // 2)
            for half in range(2):
                stats(0, UNITS, half)
                dve.wait_ge(stats_done, 2 * UNITS + half + 1)
                aggregate(half)
            dve.wait_ge(norm_T, 2 * UNITS)
            normalise(0, UNITS, 0)
            normalise(0, UNITS, 1)
            norm_lo(UNITS, 0)
            norm_lo(UNITS, 1)
            ff_unit(0)
            with dve.Fori(1, UNITS - 1) as w:
                ff_unit(w)
            ff_unit(UNITS - 1, nxt=False)


_INS = ["x", "adj"] + ["L0_gnn_" + n for n in (
    "Wq", "bq", "Wk", "bk", "Wv", "bv", "Wo", "bo", "g1", "b1", "g2", "b2", "Wf1", "bf1", "Wf2", "bf2")]


def kernel(**inputs):
    import numpy as _np
    import concourse.bacc as _bacc
    from concourse import mybir as _mybir
    from concourse.bass_utils import run_bass_kernel_spmd as _run

    nc = _bacc.Bacc("TRN2", target_bir_lowering=False, num_devices=1)
    arrays, args = {}, []
    for name in _INS:
        a = _np.ascontiguousarray(inputs[name])
        arrays[f"in_{name}"] = a
        args.append(nc.dram_tensor(f"in_{name}", a.shape, _mybir.dt.from_np(a.dtype), kind="ExternalInput").ap())
    shape = inputs["x"].shape
    args.append(nc.dram_tensor("out", shape, _mybir.dt.float32, kind="ExternalOutput").ap())
    gnn_layer(nc, *args)
    r = _run(nc, [arrays], core_ids=[0])
    return r.results[0]["out"]
```

```python
import math
from contextlib import ExitStack

import concourse.bass as bass
from concourse import mybir

F32 = mybir.dt.float32
F16 = mybir.dt.float16
BF16 = mybir.dt.bfloat16
ACT = mybir.ActivationFunctionType
ALU = mybir.AluOpType
AX = mybir.AxisListType


def gnn_layer(nc, x, adj, Wq, bq, Wk, bk, Wv, bv, Wo, bo, g1, b1, g2, b2, Wf1, bf1, Wf2, bf2, out):
    B, N, D = x.shape
    FF = Wf1.shape[1]
    H = 8
    HD = D // H
    P = 128
    DC = D // P
    FC = FF // P
    U = 4
    UNITS = B // U
    T = U * N
    HC = P // HD
    VW = HD + 2
    WS = 16.0
    LN_EPS = 1e-5
    GUARD = 1e-6
    QS = WS * float(HD) ** -0.5
    EXP_SCALE = 1.0 / (WS * WS)
    assert N == P and T == 512 and UNITS % 2 == 0

    ctx = ExitStack()
    with ctx:
        def sb(name, shape, dt=F32):
            return ctx.enter_context(nc.sbuf_tensor(name, shape, dt))

        def bank(name):
            return ctx.enter_context(nc.psum_tensor(name, [P, 512], F32))

        def sem(name):
            return ctx.enter_context(nc.semaphore(name))

        hid = sb("hid", [P, B, D])
        w_qkvo = {n: (sb(f"w{n}_hi", [P, DC, D], F16), sb(f"w{n}_lo", [P, DC, D], F16)) for n in "qkvo"}
        wf1_hi, wf1_lo = sb("wf1_hi", [P, DC, FF], F16), sb("wf1_lo", [P, DC, FF], F16)
        wf2_hi, wf2_lo = sb("wf2_hi", [P, FC, D], F16), sb("wf2_lo", [P, FC, D], F16)
        ln_cols = sb("ln_cols", [P, 4, DC])
        gain_q, gain_kv, gain_f1 = sb("gain_q", [P, DC]), sb("gain_kv", [P, DC]), sb("gain_f1", [P, DC])
        bias_cols = sb("bias_cols", [P, 4 + FC])
        bias_folded = sb("bias_folded", [P, 4 + FC])
        bv_row, bo_row, bf2_row = sb("bv_row", [P, D]), sb("bo_row", [P, D]), sb("bf2_row", [P, D])
        bv_parts = sb("bv_parts", [P, D], F16)
        bv_pick = sb("bv_pick", [P, P], F16)
        ident = sb("ident", [P, P])
        ident_bf = sb("ident_bf", [P, P], BF16)
        two_ident = sb("two_ident", [P, P], F16)
        ones_col = sb("ones_col", [P, 2], BF16)
        log_guard = sb("log_guard", [P, 1])
        minus_one = sb("minus_one", [P, U])
        minus_half = sb("minus_half", [P, U])
        eps = sb("eps", [P, U])
        nrm = sb("nrm", [P, U, D])
        bn = sb("bn", [P, U, 6])
        mv = sb("mv", [P, U, 2])
        var_eps = sb("var_eps", [P, U])
        rstd = sb("rstd", [P, U])
        minus_mean = sb("minus_mean", [P, U])
        offset = sb("offset", [P, U])
        nT_hi, nT_lo = sb("nT_hi", [P, DC, T], F16), sb("nT_lo", [P, DC, T], F16)
        adj_sb = sb("adj_sb", [P, U, P])
        adj_hi = [sb(f"adj_hi{p}", [P, U, P], F16) for p in range(2)]
        adjT_hi = sb("adjT_hi", [P, U * P], F16)
        adj_rest = sb("adj_rest", [P, U * P])
        rest_exp = sb("rest_exp", [P, U * P])
        mix = sb("mix", [P, U * P])
        quarter = sb("quarter", [P, 1])
        weight = [sb(f"weight{p}", [P, U, P]) for p in range(2)]
        qT = sb("qT", [P, 2, DC, T], F16)
        spread = sb("spread", [P, 2, HC, 2, DC, T], F16)
        kT = [(sb(f"kT_hi{p}", [P, DC, T], F16), sb(f"kT_lo{p}", [P, DC, T], F16)) for p in range(2)]
        v = [(sb(f"v_hi{p}", [P, U, H, VW], F16), sb(f"v_lo{p}", [P, U, H, VW], F16)) for p in range(2)]
        shift = sb("shift", [P, H], BF16)
        W1 = H * P
        scratch = sb("scratch", [P, 7 * W1])
        e32 = [scratch[:, p * W1:(p + 1) * W1] for p in range(2)]
        p32 = [scratch[:, (2 + p) * W1:(3 + p) * W1] for p in range(2)]
        halves = scratch[:, 4 * W1:7 * W1].bitcast(F16)
        p_hi = [halves[:, p * W1:(p + 1) * W1] for p in range(2)]
        p_lo = [halves[:, (2 + p) * W1:(3 + p) * W1] for p in range(2)]
        e_guard = [halves[:, (4 + p) * W1:(5 + p) * W1].bitcast(BF16) for p in range(2)]
        raw = scratch[:, 0:4 * DC * D].rearrange("p (w c n) -> p w c n", w=4, c=DC)
        raw_ff = spread[:, 0, :, :, :, :].rearrange("p r l c t -> p (r l c t)").bitcast(F32)
        raw_f1 = raw_ff[:, 0:DC * FF].rearrange("p (c n) -> p c n", c=DC)
        raw_f2 = raw_ff[:, DC * FF:DC * FF + FC * D].rearrange("p (c n) -> p c n", c=FC)
        denom, recip = sb("denom", [P, H]), sb("recip", [P, H])
        att = sb("att", [P, U, D])
        aT_hi, aT_lo = sb("aT_hi", [P, DC, 2 * N], F16), sb("aT_lo", [P, DC, 2 * N], F16)
        flat = spread[:, :, :, :, :, :].rearrange("p a r l c t -> p (a r l c t)")
        h32 = flat[:, 0:2 * 4 * T].bitcast(F32).rearrange("p (f t) -> p f t", t=T)
        h_hi = flat[:, 8 * T:(8 + FC) * T].rearrange("p (f t) -> p f t", t=T)
        h_lo = flat[:, (8 + FC) * T:(8 + 2 * FC) * T].rearrange("p (f t) -> p f t", t=T)

        front = [bank("front0"), bank("front1")]
        rough = ctx.enter_context(nc.psum_tensor("rough", [P, 1024], F32))
        logit = ctx.enter_context(nc.psum_tensor("logit", [P, 1024], F32))
        mixed = bank("mixed")
        back = bank("back")
        hbank = [rough[:, 0:512], rough[:, 512:1024], logit[:, 0:512], logit[:, 512:1024]]
        obank = [mixed, back]

        x_loaded = sem("x_loaded")
        adj_loaded = sem("adj_loaded")
        w_loaded = [sem(f"w_loaded_{n}") for n in ("q", "k", "v", "o", "f1", "f2")]
        small_loaded = sem("small_loaded")
        ident_set = sem("ident_set")
        consts_set = sem("consts_set")
        bias_made = sem("bias_made")
        gains_set = sem("gains_set")
        w_hi_made = sem("w_hi_made")
        w_made = sem("w_made")
        bias_sum = sem("bias_sum")
        bias_ready = sem("bias_ready")
        f1_bias_made = sem("f1_bias_made")
        f1_bias_ready = sem("f1_bias_ready")
        stats_done = sem("stats_done")
        moments = sem("moments")
        eps_added = sem("eps_added")
        rstd_ready = sem("rstd_ready")
        offset_ready = sem("offset_ready")
        normed = sem("normed")
        bias_added = sem("bias_added")
        norm_T = sem("norm_T")
        norm_T_hi = sem("norm_T_hi")
        norm_T_lo = sem("norm_T_lo")
        adj_T = sem("adj_T")
        adj_hi_ready = sem("adj_hi_ready")
        mix_ready = sem("mix_ready")
        rest_ready = sem("rest_ready")
        rest_exp_ready = sem("rest_exp_ready")
        weight_ready = sem("weight_ready")
        qk = sem("qk")
        qk_hi = sem("qk_hi")
        qk_lo = sem("qk_lo")
        val = sem("val")
        val_hi = sem("val_hi")
        val_lo = sem("val_lo")
        q_spread = sem("q_spread")
        rough_done = sem("rough_done")
        shift_ready = sem("shift_ready")
        logit_done = sem("logit_done")
        exp_ready = sem("exp_ready")
        p_ready = sem("p_ready")
        p_hi_ready = sem("p_hi_ready")
        p_lo_ready = sem("p_lo_ready")
        guard_ready = sem("guard_ready")
        mixed_done = sem("mixed_done")
        denom_ready = sem("denom_ready")
        recip_ready = sem("recip_ready")
        att_ready = sem("att_ready")
        att_T = sem("att_T")
        att_T_hi = sem("att_T_hi")
        att_T_lo = sem("att_T_lo")
        proj_done = sem("proj_done")
        resid_done = sem("resid_done")
        ff1_done = sem("ff1_done")
        gelu_done = sem("gelu_done")
        h_hi_ready = sem("h_hi_ready")
        h_lo_ready = sem("h_lo_ready")
        ff2_done = sem("ff2_done")
        out_ready = sem("out_ready")
        stored = sem("stored")

        block = ctx.enter_context(nc.Block())

        def graph(ap4, j):
            return ap4[:, j, :].unsqueeze(1).to_broadcast([P, H, P])

        @block.sync
        def _(sp):
            def load_x(u):
                sp.dma_start(hid[:, bass.ds(u * U, U), :],
                             x[bass.ds(u * U, U), :, :].rearrange("b p n -> p b n")).then_inc(x_loaded, 16)

            def load_adj(u):
                sp.dma_start(adj_sb[:, :, :],
                             adj[bass.ds(u * U, U), :, :].rearrange("b p n -> p b n")).then_inc(adj_loaded, 16)

            def spread_q(u, par):
                sp.wait_ge(qk_lo, u * 4 + 2)
                for r in range(HC):
                    rows = slice(r * HD, (r + 1) * HD)
                    sp.dma_start(spread[rows, par, r, :, :, :], qT[rows, :, :, :]).then_inc(q_spread, 16)

            load_x(0)
            load_adj(0)
            sp.dma_start(ln_cols[:, 0, :], g1.rearrange("(c p) -> p c", p=P),
                         allow_slow_non_contiguous=True).then_inc(small_loaded, 16)
            sp.dma_start(ln_cols[:, 1, :], b1.rearrange("(c p) -> p c", p=P),
                         allow_slow_non_contiguous=True).then_inc(small_loaded, 16)
            sp.dma_start(ln_cols[:, 2, :], g2.rearrange("(c p) -> p c", p=P),
                         allow_slow_non_contiguous=True).then_inc(small_loaded, 16)
            sp.dma_start(ln_cols[:, 3, :], b2.rearrange("(c p) -> p c", p=P),
                         allow_slow_non_contiguous=True).then_inc(small_loaded, 16)
            sp.dma_start(bias_cols[:, 0:2], bq.rearrange("(c p) -> p c", p=P),
                         allow_slow_non_contiguous=True).then_inc(small_loaded, 16)
            sp.dma_start(bias_cols[:, 2:4], bk.rearrange("(c p) -> p c", p=P),
                         allow_slow_non_contiguous=True).then_inc(small_loaded, 16)
            sp.dma_start(bias_cols[:, 4:4 + FC], bf1.rearrange("(c p) -> p c", p=P),
                         allow_slow_non_contiguous=True).then_inc(small_loaded, 16)
            for row, b in ((bv_row, bv), (bo_row, bo), (bf2_row, bf2)):
                sp.dma_start(row[:, :], b.rearrange("(a n) -> a n", a=1).to_broadcast([P, D])).then_inc(small_loaded, 16)
            sp.wait_ge(x_loaded, 16)
            load_x(1)
            sp.wait_ge(consts_set, 2)
            spread_q(0, 0)
            sp.wait_ge(x_loaded, 32)
            load_x(2)
            sp.wait_ge(adj_hi_ready, 1)
            load_adj(1)

            def unit(u, par, load=True, nxt=True):
                if load:
                    sp.wait_ge(x_loaded, u * 16 + 48)
                    load_x(u + 3)
                if nxt:
                    spread_q(u + 1, 1 - par)
                    sp.wait_ge(adj_hi_ready, u + 2)

            unit(0, 0)
            load_adj(2)
            with sp.Fori(0, UNITS // 2 - 2) as i:
                u = i * 2 + 1
                unit(u, 1)
                load_adj(u + 2)
                unit(u + 1, 0)
                load_adj(u + 3)
            unit(UNITS - 3, 1, load=False)
            load_adj(UNITS - 1)
            unit(UNITS - 2, 0, load=False)
            sp.wait_ge(logit_done, B - U)
            sp.dma_start(raw_f1, Wf1.rearrange("(c p) n -> p c n", p=P)).then_inc(w_loaded[4], 16)
            sp.dma_start(raw_f2, Wf2.rearrange("(c p) n -> p c n", p=P)).then_inc(w_loaded[5], 16)

            def store(w, n):
                sp.wait_ge(out_ready, n + 1)
                sp.dma_start(out[bass.ds(w, 2), :, :].rearrange("b p n -> p b n"),
                             hid[:, bass.ds(w, 2), :]).then_inc(stored, 16)

            with sp.Fori(0, B // 2) as n:
                store(n * 2, n)
            sp.wait_ge(stored, 16 * (B // 2))

        @block.gpsimd
        def _(pool):
            pool.memset(ident[:, :], 0.0).then_inc(ident_set, 1)
            pool.wait_ge(ident_set, 1)
            pool.affine_select(out=ident[:, :], in_=ident[:, :], compare_op=ALU.not_equal, fill=1.0,
                               base=0, pattern=[[-1, P]], channel_multiplier=1).then_inc(ident_set, 1)
            pool.memset(minus_one[:, :], -1.0)
            pool.memset(minus_half[:, :], -0.5)
            pool.memset(eps[:, :], LN_EPS)
            pool.memset(bv_pick[:, :], 0.0).then_inc(consts_set, 1)
            pool.memset(spread[:, :, :, :, :, :].rearrange("p a r l c t -> p (a r l c t)").bitcast(F32), 0.0)\
                .then_inc(consts_set, 1)

            def inv_std(n):
                pool.wait_ge(moments, n * 2 + 2)
                if not (isinstance(n, int) and n == 0):
                    pool.wait_ge(normed, n)
                pool.tensor_tensor(minus_mean[:, :], mv[:, :, 0], minus_one[:, :], ALU.mult)
                pool.tensor_tensor(var_eps[:, :], mv[:, :, 1], eps[:, :], ALU.add)\
                    .then_inc(eps_added, 1)
                pool.wait_ge(eps_added, n + 1)
                pool.tensor_tensor(rstd[:, :], var_eps[:, :], minus_half[:, :], ALU.pow).then_inc(rstd_ready, 1)
                pool.wait_ge(rstd_ready, n + 1)
                pool.tensor_tensor(offset[:, :], minus_mean[:, :], rstd[:, :], ALU.mult).then_inc(offset_ready, 1)

            def add_bias(u, n, row):
                pool.wait_ge(normed, n + 1)
                h = hid[:, bass.ds(u * U, U), :]
                pool.tensor_tensor(h, h, row[:, :].unsqueeze(1).to_broadcast([P, U, D]), ALU.add)\
                    .then_inc(bias_added, 1)

            def weight_of(u, par):
                pool.wait_ge(rest_exp_ready, u + 1)
                if not (isinstance(u, int) and u < 2):
                    pool.wait_ge(p_ready, u * U - U)
                pool.tensor_tensor(weight[par][:, :, :].rearrange("p b q -> p (b q)"), mix[:, :], rest_exp[:, :],
                                   ALU.mult).then_inc(weight_ready, 1)

            inv_std(0)
            pool.wait_ge(small_loaded, 160)
            add_bias(0, 0, bo_row)
            weight_of(0, 0)
            inv_std(1)
            add_bias(1, 1, bo_row)

            def unit(u, par, nxt=True, ahead=True):
                if nxt:
                    weight_of(u + 1, 1 - par)
                if ahead:
                    inv_std(u + 2)
                    add_bias(u + 2, u + 2, bo_row)

            unit(0, 0)
            with pool.Fori(0, UNITS // 2 - 2) as i:
                u = i * 2 + 1
                unit(u, 1)
                unit(u + 1, 0)
            unit(UNITS - 3, 1)
            unit(UNITS - 2, 0, ahead=False)

            with pool.Fori(0, UNITS) as w:
                inv_std(w + UNITS)
                add_bias(w, w + UNITS, bf2_row)

        @block.scalar
        def _(act):
            for n, src in enumerate((Wq, Wk, Wv, Wo)):
                act.dma_start(raw[:, n, :, :], src.rearrange("(c p) n -> p c n", p=P)).then_inc(w_loaded[n], 16)

            def normalise(u, n, js):
                if js[0] == 0:
                    act.wait_ge(offset_ready, n + 1)
                    if not (isinstance(n, int) and n == 0):
                        act.wait_ge(norm_T, n * 2)
                for j in js:
                    ins = act.activation(nrm[:, j, :], hid[:, bass.ds(u * U + j, 1), :].rearrange("p a n -> p (a n)"),
                                         ACT.Identity, bias=offset[:, j:j + 1], scale=rstd[:, j:j + 1])
                if js[-1] == U - 1:
                    ins.then_inc(normed, 1)

            def norm_hi(n, c):
                act.wait_ge(norm_T, n * 2 + c + 1)
                act.activation(nT_hi[:, c, :], front[c][:, :], ACT.Copy).then_inc(norm_T_hi, 1)

            def adjacency(u, par):
                act.wait_ge(adj_T, u + 1)
                act.activation(adj_hi[par][:, :, :].rearrange("p b k -> p (b k)"),
                               adj_sb[:, :, :].rearrange("p b k -> p (b k)"), ACT.Copy).then_inc(adj_hi_ready, 1)
                if not (isinstance(u, int) and u == 0):
                    act.wait_ge(weight_ready, u)
                act.activation(adjT_hi[:, :], front[0][:, :], ACT.Copy)
                act.activation(mix[:, :], front[0][:, :], ACT.Identity, bias=quarter[:, :], scale=0.75)\
                    .then_inc(mix_ready, 1)

            def adjacency_rest(u):
                act.wait_ge(rest_ready, u + 1)
                act.activation(rest_exp[:, :], adj_rest[:, :], ACT.Exp, scale=2.0).then_inc(rest_exp_ready, 1)

            def qk_part(u, par, m):
                if m == 0 and not (isinstance(u, int) and u == 0):
                    act.wait_ge(q_spread, u * 64)
                act.wait_ge(qk, u * 4 + m + 1)
                dst = qT[:, 0, m, :] if m < 2 else kT[par][0][:, m - 2, :]
                act.activation(dst, front[1 - m % 2][:, :], ACT.Identity,
                               bias=bias_folded[:, m:m + 1]).then_inc(qk_hi, 1)

            def val_part(u, par, m):
                act.wait_ge(val, u * 2 + m + 1)
                act.activation(v[par][0][:, 2 * m:2 * m + 2, :, 0:HD].rearrange("p b h d -> p (b h) d"),
                               front[1 - m][:, :].rearrange("p (g d) -> p g d", d=HD),
                               ACT.Copy).then_inc(val_hi, 1)

            def piece(u, par, k):
                if k == 0:
                    norm_hi(u, 0)
                    norm_hi(u, 1)
                elif k == 1:
                    adjacency(u, par)
                elif k < 6:
                    qk_part(u, par, k - 2)
                    if k == 2:
                        adjacency_rest(u)
                else:
                    val_part(u, par, k - 6)

            def part_of_p(b, s):
                act.wait_ge(p_ready, b + 1)
                if not (isinstance(b, int) and b < 2):
                    act.wait_ge(mixed_done, b - 1)
                act.activation(p_hi[s], p32[s], ACT.Copy).then_inc(p_hi_ready, 1)

            def att_part(p):
                act.wait_ge(att_T, p + 1)
                act.activation(aT_hi[:, :, :].rearrange("p c t -> p (c t)"), back[:, :], ACT.Copy)\
                    .then_inc(att_T_hi, 1)

            def exponent(b, s):
                act.wait_ge(logit_done, b + 1)
                if not (isinstance(b, int) and b < 2):
                    act.wait_ge(p_ready, b - 1)
                act.activation(e32[s], logit[:, :], ACT.Exp, scale=EXP_SCALE).then_inc(exp_ready, 1)
                if not (isinstance(b, int) and b < 2):
                    act.wait_ge(mixed_done, b - 1)
                act.activation(e_guard[s], logit[:, :], ACT.Exp, bias=log_guard[:, :], scale=EXP_SCALE)\
                    .then_inc(guard_ready, 1)

            def weight_hi(n, dst, src, gain):
                act.wait_ge(w_loaded[n], 16)
                if isinstance(gain, float):
                    ins = act.activation(dst[:, :, :], src, ACT.Copy, scale=gain)
                else:
                    for c in range(DC):
                        ins = act.activation(dst[:, c, :], src[:, c, :], ACT.Copy, scale=gain[:, c:c + 1])
                ins.then_inc(w_hi_made, 1)

            act.wait_ge(gains_set, 1)
            weight_hi(0, w_qkvo["q"][0], raw[:, 0, :, :], gain_q)
            weight_hi(1, w_qkvo["k"][0], raw[:, 1, :, :], gain_kv)
            normalise(0, 0, range(U))
            weight_hi(2, w_qkvo["v"][0], raw[:, 2, :, :], gain_kv)
            weight_hi(3, w_qkvo["o"][0], raw[:, 3, :, :], WS)
            piece(0, 0, 0)
            piece(0, 0, 1)
            act.wait_ge(bias_ready, 1)
            for k in range(2, 8):
                piece(0, 0, k)
            normalise(1, 1, range(U))

            def unit(u, par, first=False, nxt=True, ahead=True):
                for j in range(U):
                    b = u * U + j
                    if not nxt and j == 0:
                        weight_hi(4, wf1_hi, raw_f1, gain_f1)
                    if not nxt and j == 1:
                        weight_hi(5, wf2_hi, raw_f2, WS)
                    exponent(b, j % 2)
                    part_of_p(b, j % 2)
                    if nxt:
                        piece(u + 1, 1 - par, 2 * j)
                    if j == 1 and not first:
                        att_part(u * 2 - 1)
                    if j == 3:
                        att_part(u * 2)
                    if nxt:
                        piece(u + 1, 1 - par, 2 * j + 1)
                    if j >= 2 and ahead:
                        normalise(u + 2, u + 2, (2 * j - 4, 2 * j - 3))

            unit(0, 0, first=True)
            with act.Fori(0, UNITS // 2 - 2) as i:
                u = i * 2 + 1
                unit(u, 1)
                unit(u + 1, 0)
            unit(UNITS - 3, 1)
            unit(UNITS - 2, 0, ahead=False)
            unit(UNITS - 1, 1, nxt=False, ahead=False)
            att_part(B // 2 - 1)

            def gelu(w, f):
                act.wait_ge(ff1_done, w * FC + f + 1)
                if f >= 4 or not (isinstance(w, int) and w == 0):
                    act.wait_ge(h_lo_ready, w * FC + f - 3)
                if f == 0 and not (isinstance(w, int) and w == 0):
                    act.wait_ge(ff2_done, w * 2)
                act.activation(h32[:, f % 4, :], hbank[f % 4], ACT.Gelu,
                               bias=bias_folded[:, 4 + f:5 + f], scale=1.0 / WS).then_inc(gelu_done, 1)
                act.wait_ge(gelu_done, w * FC + f + 1)
                act.activation(h_hi[:, f, :], h32[:, f % 4, :], ACT.Copy).then_inc(h_hi_ready, 1)

            def ff_unit(w, nxt=True):
                for f in range(FC):
                    gelu(w, f)
                if nxt:
                    normalise(w + 1, w + UNITS + 1, range(U))
                    norm_hi(w + UNITS + 1, 0)
                    norm_hi(w + UNITS + 1, 1)

            act.wait_ge(resid_done, B // 2)
            normalise(0, UNITS, range(U))
            act.wait_ge(w_made, 6)
            act.wait_ge(f1_bias_ready, 1)
            norm_hi(UNITS, 0)
            norm_hi(UNITS, 1)
            ff_unit(0)
            with act.Fori(1, UNITS - 1) as w:
                ff_unit(w)
            ff_unit(UNITS - 1, nxt=False)

        @block.tensor
        def _(pe):
            def shift_times(dst, w, shift_col, cols):
                for k in range(DC):
                    mm = pe.matmul(dst, w[:, k, cols], ln_cols[:, shift_col, k:k + 1],
                                   start=(k == 0), stop=(k == DC - 1))
                return mm

            def chunk(f):
                return slice(f * P, (f + 1) * P)

            pe.wait_ge(small_loaded, 160)
            for n in range(3):
                pe.wait_ge(w_loaded[n], 16)
            for n in range(4):
                shift_times(mixed[:, n:n + 1], raw[:, n // 2, :, :], 1, chunk(n % 2))
            for k in range(DC):
                mm = pe.matmul(back[:, 0:D], ln_cols[:, 1, k:k + 1].to_broadcast([P, P]), raw[:, 2, k, :],
                               start=(k == 0), stop=(k == DC - 1))
            mm.then_inc(bias_made, 1)
            pe.wait_ge(ident_set, 2)

            def products(parts):
                return [(l, r) for lh, ll, rh, rl in parts for l, r in ((lh, rh), (lh, rl), (ll, rh))]

            def accumulate(dst, pairs):
                for n, (lhs, rhs) in enumerate(pairs):
                    mm = pe.matmul(dst, lhs, rhs, start=(n == 0), stop=(n == len(pairs) - 1))
                return mm

            def norm_transposes(n, c):
                if c == 0:
                    pe.wait_ge(normed, n + 1)
                for j in range(U):
                    mm = pe.transpose(front[c][:, j * P:(j + 1) * P], nrm[:, j, c * P:(c + 1) * P], ident[:, :])
                mm.then_inc(norm_T, 1)

            def piece(u, par, k):
                if k == 0:
                    for c in range(DC):
                        if not (isinstance(u, int) and u == 0):
                            pe.wait_ge(val_lo, u * 2 - c)
                        norm_transposes(u, c)
                elif k == 1:
                    pe.wait_ge(norm_T_lo, u * 2 + 1)
                    pe.wait_ge(adj_loaded, u * 16 + 16)
                    for j in range(U):
                        mm = pe.transpose(front[0][:, j * P:(j + 1) * P], adj_sb[:, j, :], ident[:, :])
                    mm.then_inc(adj_T, 1)
                elif k < 6:
                    m = k - 2
                    if m == 0:
                        pe.wait_ge(norm_T_lo, u * 2 + 2)
                    elif m == 1:
                        pe.wait_ge(rest_ready, u + 1)
                    else:
                        pe.wait_ge(qk_lo, u * 4 + m - 1)
                    w_hi, w_lo = w_qkvo["qk"[m // 2]]
                    cols = slice((m % 2) * P, (m % 2 + 1) * P)
                    accumulate(front[1 - m % 2][:, :],
                               products([(w_hi[:, c, cols], w_lo[:, c, cols], nT_hi[:, c, :], nT_lo[:, c, :])
                                         for c in range(DC)])).then_inc(qk, 1)
                else:
                    m = k - 6
                    pe.wait_ge(qk_lo, u * 4 + 3 + m)
                    w_hi, w_lo = w_qkvo["v"]
                    for jj in range(2):
                        tok = slice((2 * m + jj) * P, (2 * m + jj + 1) * P)
                        mm = accumulate(front[1 - m][:, jj * D:(jj + 1) * D],
                                        products([(nT_hi[:, c, tok], nT_lo[:, c, tok], w_hi[:, c, :], w_lo[:, c, :])
                                                  for c in range(DC)]) + [(bv_pick[:, :], bv_parts[:, :])])
                    mm.then_inc(val, 1)

            def rough_logits(u, j, par):
                b = u * U + j
                if j == 0:
                    pe.wait_ge(q_spread, u * 64 + 64)
                    pe.wait_ge(qk_lo, u * 4 + 4)
                if not (isinstance(b, int) and b == 0):
                    pe.wait_ge(shift_ready, b)
                tok = slice(j * P, (j + 1) * P)
                for h in range(H):
                    c, r = divmod(h, HC)
                    mm = pe.matmul(rough[:, h * P:(h + 1) * P], spread[:, par, r, 0, c, tok],
                                   kT[par][0][:, c, tok], start=True, stop=True)
                mm.then_inc(rough_done, 1)

            def logits(u, j, par):
                b = u * U + j
                if not (isinstance(b, int) and b == 0):
                    pe.wait_ge(guard_ready, b)
                if j == 0:
                    pe.wait_ge(adj_hi_ready, u + 1)
                tok = slice(j * P, (j + 1) * P)
                for c in range(DC):
                    k_hi, k_lo = kT[par][0][:, c, tok], kT[par][1][:, c, tok]
                    q_hi, q_lo = spread[:, par, :, 0, c, tok], spread[:, par, :, 1, c, tok]
                    adjacency = (adj_hi[par][:, j, :], two_ident[:, :].unsqueeze(1).to_broadcast([P, HC, P]))
                    for n, (lhs, rhs) in enumerate(((k_hi, q_hi), (k_hi, q_lo), (k_lo, q_hi), adjacency)):
                        pe.matmul(logit[:, c * HC * P:(c + 1) * HC * P].rearrange("p (r q) -> p r q", q=P),
                                  lhs, rhs, start=(n == 0), stop=False)
                pe.wait_ge(shift_ready, b + 1)
                for h in range(H):
                    mm = pe.matmul(logit[:, h * P:(h + 1) * P], shift[:, h:h + 1].to_broadcast([P, P]),
                                   ident_bf[:, :], start=False, stop=(h % HC == HC - 1))
                mm.then_inc(logit_done, 1)

            def mix_values(b, j, par, check_v):
                pe.wait_ge(guard_ready, b + 1)
                pe.wait_ge(p_lo_ready, b + 1)
                if check_v is not None:
                    pe.wait_ge(val_lo, check_v)
                if not (isinstance(b, int) and b == 0):
                    pe.wait_ge(att_ready, b)
                s = j % 2
                v_hi, v_lo = v[par]
                for h in range(H):
                    cols = slice(h * P, (h + 1) * P)
                    accumulate(mixed[:, h * VW:h * VW + HD + 1],
                               [(p_hi[s][:, cols], v_hi[:, j, h, 0:HD + 1]), (p_hi[s][:, cols], v_lo[:, j, h, 0:HD + 1]),
                                (p_lo[s][:, cols], v_hi[:, j, h, 0:HD + 1])])
                for h in range(H):
                    mm = pe.matmul(mixed[:, h * VW + HD + 1:(h + 1) * VW], e_guard[s][:, h * P:(h + 1) * P],
                                   ones_col[:, 0:1], start=True, stop=True)
                mm.then_inc(mixed_done, 1)

            def att_transposes(p, s):
                pe.wait_ge(att_ready, p * 2 + 2)
                if not (isinstance(p, int) and p == 0):
                    pe.wait_ge(resid_done, p)
                for c in range(DC):
                    for jj in range(2):
                        mm = pe.transpose(back[:, (c * 2 + jj) * P:(c * 2 + jj + 1) * P],
                                          att[:, s + jj, c * P:(c + 1) * P], ident[:, :])
                mm.then_inc(att_T, 1)

            def project(p):
                pe.wait_ge(att_T_lo, p + 1)
                w_hi, w_lo = w_qkvo["o"]
                for jj in range(2):
                    tok = slice(jj * P, (jj + 1) * P)
                    mm = accumulate(back[:, jj * D:(jj + 1) * D],
                                    products([(aT_hi[:, c, tok], aT_lo[:, c, tok], w_hi[:, c, :], w_lo[:, c, :])
                                              for c in range(DC)]))
                mm.then_inc(proj_done, 1)

            piece(0, 0, 0)
            piece(0, 0, 1)
            for k in range(2, 8):
                if k % 2 == 0:
                    pe.wait_ge(w_made, k // 2)
                piece(0, 0, k)
            rough_logits(0, 0, 0)
            pe.wait_ge(w_made, 4)

            def unit(u, par, first=False, nxt=True):
                for j in range(U):
                    b = u * U + j
                    logits(u, j, par)
                    if j < U - 1:
                        rough_logits(u, j + 1, par)
                    elif nxt:
                        rough_logits(u + 1, 0, 1 - par)
                    if j > 0:
                        mix_values(b - 1, j - 1, par, u * 2 + 2 if j == 1 else None)
                    elif not first:
                        mix_values(b - 1, U - 1, 1 - par, None)
                    if nxt:
                        piece(u + 1, 1 - par, 2 * j)
                    if j == 0 and not first:
                        project(u * 2 - 2)
                    if j == 1 and not first:
                        att_transposes(u * 2 - 1, 2)
                    if j == 2 and not first:
                        project(u * 2 - 1)
                    if j == 3:
                        att_transposes(u * 2, 0)
                    if nxt:
                        piece(u + 1, 1 - par, 2 * j + 1)
                    if not nxt and j == 0:
                        pe.wait_ge(w_loaded[4], 16)
                        pe.wait_ge(val_lo, 2 * UNITS)
                        for f in range(FC):
                            mm = shift_times(front[0][:, f:f + 1], raw_f1, 3, chunk(f))
                        mm.then_inc(f1_bias_made, 1)

            unit(0, 0, first=True)
            with pe.Fori(0, UNITS // 2 - 2) as i:
                u = i * 2 + 1
                unit(u, 1)
                unit(u + 1, 0)
            unit(UNITS - 3, 1)
            unit(UNITS - 2, 0)
            unit(UNITS - 1, 1, nxt=False)
            project(B // 2 - 2)
            mix_values(B - 1, U - 1, 1, None)
            att_transposes(B // 2 - 1, 2)
            project(B // 2 - 1)

            def ff1(w, f):
                if f >= 4 or not (isinstance(w, int) and w == 0):
                    pe.wait_ge(gelu_done, w * FC + f - 3)
                cols = slice(f * P, (f + 1) * P)
                accumulate(hbank[f % 4],
                           products([(wf1_hi[:, c, cols], wf1_lo[:, c, cols], nT_hi[:, c, :], nT_lo[:, c, :])
                                     for c in range(DC)])).then_inc(ff1_done, 1)

            def ff2(w, m):
                if m == 0 and not (isinstance(w, int) and w == 0):
                    pe.wait_ge(out_ready, w * 2 - 1)
                if m == 1 and not (isinstance(w, int) and w == 0):
                    pe.wait_ge(out_ready, w * 2)
                for jj in range(2):
                    tok = slice((2 * m + jj) * P, (2 * m + jj + 1) * P)
                    for f in range(FC):
                        if m == 0 and jj == 0:
                            pe.wait_ge(h_lo_ready, w * FC + f + 1)
                        for n, (lhs, rhs) in enumerate(products(
                                [(h_hi[:, f, tok], h_lo[:, f, tok], wf2_hi[:, f, :], wf2_lo[:, f, :])])):
                            mm = pe.matmul(obank[m][:, jj * D:(jj + 1) * D], lhs, rhs,
                                           start=(f == 0 and n == 0), stop=(f == FC - 1 and n == 2))
                mm.then_inc(ff2_done, 1)

            def ff_unit(w, nxt=True):
                pe.wait_ge(norm_T_lo, w * 2 + 2 * UNITS + 2)
                for f in range(FC):
                    ff1(w, f)
                ff2(w, 0)
                if nxt:
                    norm_transposes(w + UNITS + 1, 0)
                    norm_transposes(w + UNITS + 1, 1)
                ff2(w, 1)

            pe.wait_ge(f1_bias_ready, 1)
            norm_transposes(UNITS, 0)
            norm_transposes(UNITS, 1)
            pe.wait_ge(w_made, 6)
            pe.wait_ge(guard_ready, B)
            pe.wait_ge(shift_ready, B)
            pe.wait_ge(resid_done, B // 2)
            ff_unit(0)
            with pe.Fori(1, UNITS - 1) as w:
                ff_unit(w)
            ff_unit(UNITS - 1, nxt=False)

        @block.vector
        def _(dve):
            dve.memset(quarter[:, :], 0.25)
            dve.memset(log_guard[:, :], math.log(GUARD))
            dve.memset(ones_col[:, :], 1.0)
            for p in range(2):
                dve.memset(v[p][0][:, :, :, HD:VW], 1.0)
                dve.memset(v[p][1][:, :, :, HD:VW], 0.0)
            dve.wait_ge(ident_set, 2)
            dve.tensor_copy(ident_bf[:, :], ident[:, :])
            dve.tensor_scalar(two_ident[:, :], ident[:, :], 2.0 / EXP_SCALE, None, ALU.mult)
            dve.wait_ge(consts_set, 1)
            dve.memset(bv_pick[0:1, :], 1.0)
            dve.memset(bv_pick[32:33, :], 1.0)

            def stats(u, n, half):
                for j in (2 * half, 2 * half + 1):
                    ins = dve.bn_stats(bn[:, j, :], hid[:, bass.ds(u * U + j, 1), :].rearrange("p a n -> p (a n)"))
                ins.then_inc(stats_done, 1)

            def aggregate(half):
                for j in (2 * half, 2 * half + 1):
                    ins = dve.bn_aggr(mv[:, j, :], bn[:, j, :])
                ins.then_inc(moments, 1)

            dve.wait_ge(x_loaded, 16)
            stats(0, 0, 0)
            dve.wait_ge(stats_done, 1)
            aggregate(0)
            stats(0, 0, 1)
            dve.wait_ge(stats_done, 2)
            aggregate(1)

            dve.wait_ge(small_loaded, 160)
            dve.tensor_scalar(gain_q[:, :], ln_cols[:, 0, :], QS, None, ALU.mult)
            dve.tensor_scalar(gain_kv[:, :], ln_cols[:, 0, :], WS, None, ALU.mult)
            dve.tensor_scalar(gain_f1[:, :], ln_cols[:, 2, :], WS, None, ALU.mult).then_inc(gains_set, 1)
            dve.wait_ge(gains_set, 1)

            def weight_lo(n, hi, lo, src, gain):
                dve.wait_ge(w_hi_made, n + 1)
                if isinstance(gain, float):
                    ins = dve.scalar_tensor_tensor(lo[:, :, :], src, gain, hi[:, :, :], ALU.mult, ALU.subtract)
                else:
                    for c in range(DC):
                        ins = dve.scalar_tensor_tensor(lo[:, c, :], src[:, c, :], gain[:, c:c + 1], hi[:, c, :],
                                                       ALU.mult, ALU.subtract)
                ins.then_inc(w_made, 1)

            weight_lo(0, *w_qkvo["q"], raw[:, 0, :, :], gain_q)
            weight_lo(1, *w_qkvo["k"], raw[:, 1, :, :], gain_kv)

            dve.wait_ge(bias_made, 1)
            dve.tensor_tensor(bias_folded[:, 0:4], mixed[:, 0:4], bias_cols[:, 0:4], ALU.add)
            dve.tensor_tensor(bv_row[:, :], back[:, 0:D], bv_row[:, :], ALU.add).then_inc(bias_sum, 1)
            dve.wait_ge(bias_sum, 1)
            dve.tensor_scalar(bias_folded[:, 0:2], bias_folded[:, 0:2], QS, None, ALU.mult)
            dve.tensor_scalar(bias_folded[:, 2:4], bias_folded[:, 2:4], WS, None, ALU.mult)
            dve.tensor_scalar(bv_row[:, :], bv_row[:, :], WS, None, ALU.mult).then_inc(bias_sum, 1)
            dve.wait_ge(bias_sum, 2)
            dve.tensor_copy(bv_parts[:, :], bv_row[:, :]).then_inc(bias_sum, 1)
            dve.wait_ge(bias_sum, 3)
            dve.tensor_tensor(bv_parts[32:64, :], bv_row[32:64, :], bv_parts[32:64, :], ALU.subtract)\
                .then_inc(bias_ready, 1)
            weight_lo(2, *w_qkvo["v"], raw[:, 2, :, :], gain_kv)

            def norm_lo(n, c):
                dve.wait_ge(norm_T_hi, n * 2 + c + 1)
                dve.tensor_tensor(nT_lo[:, c, :], front[c][:, :], nT_hi[:, c, :], ALU.subtract)\
                    .then_inc(norm_T_lo, 1)

            def adjacency_rest(u):
                dve.wait_ge(mix_ready, u + 1)
                dve.tensor_tensor(adj_rest[:, :], front[0][:, :], adjT_hi[:, :], ALU.subtract)\
                    .then_inc(rest_ready, 1)

            def qk_part(u, par, m):
                dve.wait_ge(qk_hi, u * 4 + m + 1)
                hi = qT[:, 0, m, :] if m < 2 else kT[par][0][:, m - 2, :]
                lo = qT[:, 1, m, :] if m < 2 else kT[par][1][:, m - 2, :]
                dve.scalar_tensor_tensor(lo, front[1 - m % 2][:, :], bias_folded[:, m:m + 1], hi,
                                         ALU.add, ALU.subtract).then_inc(qk_lo, 1)

            def val_part(u, par, m):
                dve.wait_ge(val_hi, u * 2 + m + 1)
                part = [v[par][i][:, 2 * m:2 * m + 2, :, 0:HD].rearrange("p b h d -> p (b h) d") for i in range(2)]
                dve.tensor_tensor(part[1], front[1 - m][:, :].rearrange("p (g d) -> p g d", d=HD), part[0],
                                  ALU.subtract).then_inc(val_lo, 1)

            def piece(u, par, k):
                if k == 0:
                    norm_lo(u, 0)
                    norm_lo(u, 1)
                elif k == 1:
                    adjacency_rest(u)
                elif k < 6:
                    qk_part(u, par, k - 2)
                else:
                    val_part(u, par, k - 6)

            def maximum(b):
                dve.wait_ge(rough_done, b + 1)
                if not (isinstance(b, int) and b == 0):
                    dve.wait_ge(logit_done, b)
                dve.tensor_reduce(shift[:, :], rough[:, :].rearrange("p (h k) -> p h k", k=P), AX.X, ALU.max,
                                  negate=True).then_inc(shift_ready, 1)

            def weighted(u, j, par, ahead):
                b = u * U + j
                if ahead and j < 2:
                    dve.wait_ge(stats_done, u * 2 + 5 + j)
                dve.wait_ge(exp_ready, b + 1)
                if j == 0:
                    dve.wait_ge(weight_ready, u + 1)
                if not (isinstance(b, int) and b < 2):
                    dve.wait_ge(p_lo_ready, b - 1)
                dve.tensor_tensor(p32[j % 2].rearrange("p (h q) -> p h q", q=P),
                                  e32[j % 2].rearrange("p (h q) -> p h q", q=P),
                                  graph(weight[par], j), ALU.mult).then_inc(p_ready, 1)

            def part_of_p(b, s):
                dve.wait_ge(p_hi_ready, b + 1)
                dve.tensor_tensor(p_lo[s], p32[s], p_hi[s], ALU.subtract).then_inc(p_lo_ready, 1)

            per_head = mixed[:, 0:H * VW].rearrange("p (h d) -> p h d", d=VW)

            def denominator(b):
                dve.wait_ge(mixed_done, b + 1)
                dve.tensor_reduce(denom[:, :], per_head[:, :, HD:VW], AX.X, ALU.max).then_inc(denom_ready, 1)

            def reciprocal(b):
                dve.wait_ge(denom_ready, b + 1)
                dve.reciprocal(recip[:, :], denom[:, :]).then_inc(recip_ready, 1)

            def attended(b, j, transposed):
                dve.wait_ge(recip_ready, b + 1)
                if transposed is not None and j % 2 == 0:
                    dve.wait_ge(att_T, transposed)
                dve.tensor_tensor(att[:, j, :].rearrange("p (h d) -> p h d", d=HD), per_head[:, :, 0:HD],
                                  recip[:, :].unsqueeze(2).to_broadcast([P, H, HD]), ALU.mult)\
                    .then_inc(att_ready, 1)

            def att_part(p):
                dve.wait_ge(att_T_hi, p + 1)
                dve.tensor_tensor(aT_lo[:, :, :].rearrange("p c t -> p (c t)"), back[:, :],
                                  aT_hi[:, :, :].rearrange("p c t -> p (c t)"), ALU.subtract).then_inc(att_T_lo, 1)

            def residual(p, b):
                dve.wait_ge(proj_done, p + 1)
                h = hid[:, bass.ds(b, 2), :].rearrange("p a n -> p (a n)")
                dve.scalar_tensor_tensor(h, back[:, :], 1.0 / (WS * WS), h, ALU.mult, ALU.add)\
                    .then_inc(resid_done, 1)

            for k in range(8):
                piece(0, 0, k)
            maximum(0)
            weight_lo(3, *w_qkvo["o"], raw[:, 3, :, :], WS)
            dve.wait_ge(x_loaded, 32)
            stats(1, 1, 0)
            dve.wait_ge(stats_done, 3)
            aggregate(0)
            stats(1, 1, 1)
            dve.wait_ge(stats_done, 4)
            aggregate(1)

            def unit(u, par, first=False, nxt=True, ahead=True):
                for j in range(U):
                    b = u * U + j
                    before = not (first and j == 0)
                    if j == 0 and ahead:
                        dve.wait_ge(x_loaded, u * 16 + 48)
                    if j < 2 and ahead:
                        if j == 0:
                            dve.wait_ge(offset_ready, u + 2)
                        stats(u + 2, u + 2, j)
                    weighted(u, j, par, ahead)
                    if j < 2 and ahead:
                        aggregate(j)
                    if before:
                        denominator(b - 1)
                    if nxt or j < U - 1:
                        maximum(b + 1)
                    if before:
                        reciprocal(b - 1)
                    part_of_p(b, j % 2)
                    if before:
                        attended(b - 1, (j - 1) % U,
                                 None if first else u * 2 - 1 + j // 2 if j > 0 else u * 2 - 2)
                    if nxt:
                        piece(u + 1, 1 - par, 2 * j)
                    if j == 0 and not first:
                        dve.wait_ge(bias_added, u)
                        residual(u * 2 - 2, u * U - U)
                    if j == 1 and not first:
                        att_part(u * 2 - 1)
                    if j == 2 and not first:
                        residual(u * 2 - 1, u * U - 2)
                    if j == 3:
                        att_part(u * 2)
                    if nxt:
                        piece(u + 1, 1 - par, 2 * j + 1)
                    if not nxt and j == 0:
                        weight_lo(4, wf1_hi, wf1_lo, raw_f1, gain_f1)
                        dve.wait_ge(f1_bias_made, 1)
                        dve.tensor_tensor(bias_folded[:, 4:4 + FC], front[0][:, 0:FC], bias_cols[:, 4:4 + FC], ALU.add)\
                            .then_inc(f1_bias_ready, 1)
                    if not nxt and j == 1:
                        weight_lo(5, wf2_hi, wf2_lo, raw_f2, WS)

            unit(0, 0, first=True)
            with dve.Fori(0, UNITS // 2 - 2) as i:
                u = i * 2 + 1
                unit(u, 1)
                unit(u + 1, 0)
            unit(UNITS - 3, 1)
            unit(UNITS - 2, 0, ahead=False)
            unit(UNITS - 1, 1, nxt=False, ahead=False)
            dve.wait_ge(bias_added, UNITS)
            residual(B // 2 - 2, B - 4)
            denominator(B - 1)
            reciprocal(B - 1)
            attended(B - 1, 3, None)
            att_part(B // 2 - 1)
            residual(B // 2 - 1, B - 2)

            def h_part(w, f, nxt):
                if nxt and f in (1, 3):
                    dve.wait_ge(stats_done, w * 2 + 2 * UNITS + 3 + f // 2)
                dve.wait_ge(h_hi_ready, w * FC + f + 1)
                dve.tensor_tensor(h_lo[:, f, :], h32[:, f % 4, :], h_hi[:, f, :], ALU.subtract)\
                    .then_inc(h_lo_ready, 1)

            def finish(w, m):
                dve.wait_ge(ff2_done, w * 2 + m + 1)
                dve.wait_ge(bias_added, w + UNITS + 1)
                h = hid[:, bass.ds(w * U + 2 * m, 2), :].rearrange("p a n -> p (a n)")
                dve.scalar_tensor_tensor(h, obank[m][:, :], 1.0 / WS, h, ALU.mult, ALU.add)\
                    .then_inc(out_ready, 1)

            def ff_unit(w, nxt=True):
                for f in range(FC):
                    if nxt and f in (0, 2):
                        if f == 0:
                            dve.wait_ge(offset_ready, w + UNITS + 1)
                        stats(w + 1, w + UNITS + 1, f // 2)
                    h_part(w, f, nxt)
                    if nxt and f in (1, 3):
                        aggregate(f // 2)
                if nxt:
                    norm_lo(w + UNITS + 1, 0)
                    norm_lo(w + UNITS + 1, 1)
                finish(w, 0)
                finish(w, 1)

            dve.wait_ge(resid_done, B // 2)
            for half in range(2):
                stats(0, UNITS, half)
                dve.wait_ge(stats_done, 2 * UNITS + half + 1)
                aggregate(half)
            norm_lo(UNITS, 0)
            norm_lo(UNITS, 1)
            ff_unit(0)
            with dve.Fori(1, UNITS - 1) as w:
                ff_unit(w)
            ff_unit(UNITS - 1, nxt=False)


_INS = ["x", "adj"] + ["L0_gnn_" + n for n in (
    "Wq", "bq", "Wk", "bk", "Wv", "bv", "Wo", "bo", "g1", "b1", "g2", "b2", "Wf1", "bf1", "Wf2", "bf2")]


def kernel(**inputs):
    import numpy as _np
    import concourse.bacc as _bacc
    from concourse import mybir as _mybir
    from concourse.bass_utils import run_bass_kernel_spmd as _run

    nc = _bacc.Bacc("TRN2", target_bir_lowering=False, num_devices=1)
    arrays, args = {}, []
    for name in _INS:
        a = _np.ascontiguousarray(inputs[name])
        arrays[f"in_{name}"] = a
        args.append(nc.dram_tensor(f"in_{name}", a.shape, _mybir.dt.from_np(a.dtype), kind="ExternalInput").ap())
    shape = inputs["x"].shape
    args.append(nc.dram_tensor("out", shape, _mybir.dt.float32, kind="ExternalOutput").ap())
    gnn_layer(nc, *args)
    r = _run(nc, [arrays], core_ids=[0])
    return r.results[0]["out"]
```

```python
import math
from contextlib import ExitStack

import concourse.bass as bass
from concourse import mybir

F32 = mybir.dt.float32
F16 = mybir.dt.float16
BF16 = mybir.dt.bfloat16
ACT = mybir.ActivationFunctionType
ALU = mybir.AluOpType
AX = mybir.AxisListType


def gnn_layer(nc, x, adj, Wq, bq, Wk, bk, Wv, bv, Wo, bo, g1, b1, g2, b2, Wf1, bf1, Wf2, bf2, out):
    B, N, D = x.shape
    FF = Wf1.shape[1]
    H = 8
    HD = D // H
    P = 128
    DC = D // P
    FC = FF // P
    U = 4
    UNITS = B // U
    T = U * N
    HC = P // HD
    VW = HD + 2
    WS = 16.0
    LN_EPS = 1e-5
    GUARD = 1e-6
    QS = WS * float(HD) ** -0.5
    EXP_SCALE = 1.0 / (WS * WS)
    assert N == P and T == 512 and UNITS % 2 == 0

    ctx = ExitStack()
    with ctx:
        def sb(name, shape, dt=F32):
            return ctx.enter_context(nc.sbuf_tensor(name, shape, dt))

        def bank(name):
            return ctx.enter_context(nc.psum_tensor(name, [P, 512], F32))

        def sem(name):
            return ctx.enter_context(nc.semaphore(name))

        hid = sb("hid", [P, B, D])
        w_qkvo = {n: (sb(f"w{n}_hi", [P, DC, D], F16), sb(f"w{n}_lo", [P, DC, D], F16)) for n in "qkvo"}
        wf1_hi, wf1_lo = sb("wf1_hi", [P, DC, FF], F16), sb("wf1_lo", [P, DC, FF], F16)
        wf2_hi, wf2_lo = sb("wf2_hi", [P, FC, D], F16), sb("wf2_lo", [P, FC, D], F16)
        ln_cols = sb("ln_cols", [P, 4, DC])
        gain_q, gain_kv, gain_f1 = sb("gain_q", [P, DC]), sb("gain_kv", [P, DC]), sb("gain_f1", [P, DC])
        bias_cols = sb("bias_cols", [P, 4 + FC])
        bias_folded = sb("bias_folded", [P, 4 + FC])
        bv_row, bo_row, bf2_row = sb("bv_row", [P, D]), sb("bo_row", [P, D]), sb("bf2_row", [P, D])
        bv_parts = sb("bv_parts", [P, D], F16)
        bv_pick = sb("bv_pick", [P, P], F16)
        ident = sb("ident", [P, P])
        ident_bf = sb("ident_bf", [P, P], BF16)
        two_ident = sb("two_ident", [P, P], F16)
        ones_col = sb("ones_col", [P, 2], BF16)
        log_guard = sb("log_guard", [P, 1])
        minus_one = sb("minus_one", [P, U])
        minus_half = sb("minus_half", [P, U])
        eps = sb("eps", [P, U])
        nrm = sb("nrm", [P, U, D])
        bn = sb("bn", [P, U, 6])
        mv = sb("mv", [P, U, 2])
        var_eps = sb("var_eps", [P, U])
        rstd = sb("rstd", [P, U])
        minus_mean = sb("minus_mean", [P, U])
        offset = sb("offset", [P, U])
        nT_hi, nT_lo = sb("nT_hi", [P, DC, T], F16), sb("nT_lo", [P, DC, T], F16)
        adj_sb = sb("adj_sb", [P, U, P])
        adj_hi = [sb(f"adj_hi{p}", [P, U, P], F16) for p in range(2)]
        adjT = sb("adjT", [P, U * P])
        adjT_hi = sb("adjT_hi", [P, U * P], F16)
        adj_rest = sb("adj_rest", [P, U * P])
        rest_exp = sb("rest_exp", [P, U * P])
        mix = sb("mix", [P, U * P])
        quarter = sb("quarter", [P, 1])
        weight = [sb(f"weight{p}", [P, U, P]) for p in range(2)]
        qT = sb("qT", [P, 2, DC, T], F16)
        kT = sb("kT", [P, 2, DC, T], F16)
        stack = sb("stack", [P, 2, 2, DC, HC, T], F16)
        v = [(sb(f"v_hi{p}", [P, U, H, VW], F16), sb(f"v_lo{p}", [P, U, H, VW], F16)) for p in range(2)]
        shift = sb("shift", [P, H], BF16)
        W1 = H * P
        scratch = sb("scratch", [P, 7 * W1])
        e32 = [scratch[:, p * W1:(p + 1) * W1] for p in range(2)]
        p32 = [scratch[:, (2 + p) * W1:(3 + p) * W1] for p in range(2)]
        halves = scratch[:, 4 * W1:7 * W1].bitcast(F16)
        p_hi = [halves[:, p * W1:(p + 1) * W1] for p in range(2)]
        p_lo = [halves[:, (2 + p) * W1:(3 + p) * W1] for p in range(2)]
        e_guard = [halves[:, (4 + p) * W1:(5 + p) * W1].bitcast(BF16) for p in range(2)]
        raw = scratch[:, 0:4 * DC * D].rearrange("p (w c n) -> p w c n", w=4, c=DC)
        raw_f1 = scratch[:, 4 * DC * D:4 * DC * D + DC * FF].rearrange("p (c n) -> p c n", c=DC)
        raw_f2 = scratch[:, 4 * DC * D + DC * FF:4 * DC * D + DC * FF + FC * D].rearrange("p (c n) -> p c n", c=FC)
        assert 4 * DC * D + DC * FF + FC * D <= 6 * W1
        denom, recip = sb("denom", [P, H]), sb("recip", [P, H])
        att = sb("att", [P, U, D])
        aT_hi, aT_lo = sb("aT_hi", [P, DC, 2 * N], F16), sb("aT_lo", [P, DC, 2 * N], F16)
        flat = stack[:, :, :, :, :, :].rearrange("p a m c r t -> p (a m c r t)")
        h32 = flat[:, 0:2 * 4 * T].bitcast(F32).rearrange("p (f t) -> p f t", t=T)
        h_hi = flat[:, 8 * T:(8 + FC) * T].rearrange("p (f t) -> p f t", t=T)
        h_lo = flat[:, (8 + FC) * T:(8 + 2 * FC) * T].rearrange("p (f t) -> p f t", t=T)

        front = [bank("front0"), bank("front1")]
        row_logit = ctx.enter_context(nc.psum_tensor("row_logit", [P, 1024], F32))
        logit = ctx.enter_context(nc.psum_tensor("logit", [P, 1024], F32))
        mixed = bank("mixed")
        back = bank("back")
        hbank = [row_logit[:, 0:512], row_logit[:, 512:1024], logit[:, 0:512], logit[:, 512:1024]]
        obank = [mixed, back]

        x_loaded = sem("x_loaded")
        adj_loaded = sem("adj_loaded")
        w_loaded = [sem(f"w_loaded_{n}") for n in ("q", "k", "v", "o", "f1", "f2")]
        gain1_loaded = sem("gain1_loaded")
        bias_loaded = sem("bias_loaded")
        small_loaded = sem("small_loaded")
        ident_set = sem("ident_set")
        consts_set = sem("consts_set")
        bias_made = sem("bias_made")
        gains_set = sem("gains_set")
        w_hi_made = sem("w_hi_made")
        w_made = sem("w_made")
        bias_sum = sem("bias_sum")
        bias_ready = sem("bias_ready")
        f1_bias_made = sem("f1_bias_made")
        f1_bias_ready = sem("f1_bias_ready")
        stats_done = sem("stats_done")
        moments = sem("moments")
        eps_added = sem("eps_added")
        rstd_ready = sem("rstd_ready")
        offset_ready = sem("offset_ready")
        normed = sem("normed")
        bias_added = sem("bias_added")
        norm_T = sem("norm_T")
        norm_T_hi = sem("norm_T_hi")
        norm_T_lo = sem("norm_T_lo")
        adj_T = sem("adj_T")
        adj_hi_ready = sem("adj_hi_ready")
        adjT_ready = sem("adjT_ready")
        mix_ready = sem("mix_ready")
        rest_ready = sem("rest_ready")
        rest_exp_ready = sem("rest_exp_ready")
        weight_ready = sem("weight_ready")
        qk = sem("qk")
        qk_hi = sem("qk_hi")
        qk_lo = sem("qk_lo")
        val = sem("val")
        val_hi = sem("val_hi")
        val_lo = sem("val_lo")
        q_stacked = sem("q_stacked")
        k_stacked = sem("k_stacked")
        row_done = sem("row_done")
        shift_ready = sem("shift_ready")
        logit_done = sem("logit_done")
        exp_ready = sem("exp_ready")
        p_ready = sem("p_ready")
        p_hi_ready = sem("p_hi_ready")
        p_lo_ready = sem("p_lo_ready")
        guard_ready = sem("guard_ready")
        mixed_done = sem("mixed_done")
        denom_ready = sem("denom_ready")
        recip_ready = sem("recip_ready")
        att_ready = sem("att_ready")
        att_T = sem("att_T")
        att_T_hi = sem("att_T_hi")
        att_T_lo = sem("att_T_lo")
        proj_done = sem("proj_done")
        resid_done = sem("resid_done")
        ff1_done = sem("ff1_done")
        gelu_done = sem("gelu_done")
        h_hi_ready = sem("h_hi_ready")
        h_lo_ready = sem("h_lo_ready")
        ff2_done = sem("ff2_done")
        out_ready = sem("out_ready")
        stored = sem("stored")

        block = ctx.enter_context(nc.Block())

        def front_bank(par, k):
            return front[(par + k) % 2]

        AHEAD = ((1, (5, 6)), (1, (7, 8)), (2, (0, 1)), (2, (2, 3, 4)))

        def ahead_of(u, par, j, last):
            d, pieces = AHEAD[j]
            return [(u + d, par if d == 2 else 1 - par, k) for k in pieces if d <= last or d == last + 1 and k < 2]

        def graph(ap4, j):
            return ap4[:, j, :].unsqueeze(1).to_broadcast([P, H, P])

        @block.sync
        def _(sp):
            def load_x(u):
                sp.dma_start(hid[:, bass.ds(u * U, U), :],
                             x[bass.ds(u * U, U), :, :].rearrange("b p n -> p b n")).then_inc(x_loaded, 16)

            def load_adj(u):
                sp.dma_start(adj_sb[:, :, :],
                             adj[bass.ds(u * U, U), :, :].rearrange("b p n -> p b n")).then_inc(adj_loaded, 16)

            def stack_up(u, par, m):
                sp.wait_ge(qk_lo, u * 4 + 2 * m + 2)
                for g, part in enumerate(((0, 1, 0), (0, 0, 1))[m]):
                    for r in range(HC):
                        sp.dma_start(stack[g * HD:(g + 1) * HD, par, m, :, r, :],
                                     (qT, kT)[m][r * HD:(r + 1) * HD, part, :, :])\
                            .then_inc((q_stacked, k_stacked)[m], 16)

            load_x(0)
            sp.dma_start(ln_cols[:, 0, :], g1.rearrange("(c p) -> p c", p=P),
                         allow_slow_non_contiguous=True).then_inc(gain1_loaded, 16)
            sp.dma_start(ln_cols[:, 1, :], b1.rearrange("(c p) -> p c", p=P),
                         allow_slow_non_contiguous=True).then_inc(gain1_loaded, 16)
            load_adj(0)
            sp.dma_start(bias_cols[:, 0:2], bq.rearrange("(c p) -> p c", p=P),
                         allow_slow_non_contiguous=True).then_inc(bias_loaded, 16)
            sp.dma_start(bias_cols[:, 2:4], bk.rearrange("(c p) -> p c", p=P),
                         allow_slow_non_contiguous=True).then_inc(bias_loaded, 16)
            sp.dma_start(bv_row[:, :], bv.rearrange("(a n) -> a n", a=1).to_broadcast([P, D])).then_inc(bias_loaded, 16)
            sp.wait_ge(x_loaded, 16)
            load_x(1)
            sp.dma_start(ln_cols[:, 2, :], g2.rearrange("(c p) -> p c", p=P),
                         allow_slow_non_contiguous=True).then_inc(small_loaded, 16)
            sp.dma_start(ln_cols[:, 3, :], b2.rearrange("(c p) -> p c", p=P),
                         allow_slow_non_contiguous=True).then_inc(small_loaded, 16)
            sp.dma_start(bias_cols[:, 4:4 + FC], bf1.rearrange("(c p) -> p c", p=P),
                         allow_slow_non_contiguous=True).then_inc(small_loaded, 16)
            for row, b in ((bo_row, bo), (bf2_row, bf2)):
                sp.dma_start(row[:, :], b.rearrange("(a n) -> a n", a=1).to_broadcast([P, D])).then_inc(small_loaded, 16)
            sp.dma_start(raw_f1, Wf1.rearrange("(c p) n -> p c n", p=P)).then_inc(w_loaded[4], 16)
            sp.dma_start(raw_f2, Wf2.rearrange("(c p) n -> p c n", p=P)).then_inc(w_loaded[5], 16)
            stack_up(0, 0, 0)
            sp.wait_ge(adj_hi_ready, 1)
            load_adj(1)
            stack_up(0, 0, 1)
            sp.wait_ge(x_loaded, 32)
            load_x(2)
            stack_up(1, 1, 0)

            def unit(u, par, load=True, ahead=True):
                if ahead:
                    sp.wait_ge(adj_hi_ready, u + 2)
                    load_adj(u + 2)
                stack_up(u + 1, 1 - par, 1)
                if load:
                    sp.wait_ge(x_loaded, u * 16 + 48)
                    load_x(u + 3)
                if ahead:
                    stack_up(u + 2, par, 0)

            unit(0, 0)
            with sp.Fori(0, UNITS // 2 - 2) as i:
                u = i * 2 + 1
                unit(u, 1)
                unit(u + 1, 0)
            unit(UNITS - 3, 1, load=False)
            unit(UNITS - 2, 0, load=False, ahead=False)

            def store(w, n):
                sp.wait_ge(out_ready, n + 1)
                sp.dma_start(out[bass.ds(w, 2), :, :].rearrange("b p n -> p b n"),
                             hid[:, bass.ds(w, 2), :]).then_inc(stored, 16)

            with sp.Fori(0, B // 2) as n:
                store(n * 2, n)
            sp.wait_ge(stored, 16 * (B // 2))

        @block.gpsimd
        def _(pool):
            pool.memset(ident[:, :], 0.0).then_inc(ident_set, 1)
            pool.wait_ge(ident_set, 1)
            pool.affine_select(out=ident[:, :], in_=ident[:, :], compare_op=ALU.not_equal, fill=1.0,
                               base=0, pattern=[[-1, P]], channel_multiplier=1).then_inc(ident_set, 1)
            pool.memset(minus_one[:, :], -1.0)
            pool.memset(minus_half[:, :], -0.5)
            pool.memset(eps[:, :], LN_EPS)
            pool.memset(bv_pick[:, :], 0.0).then_inc(consts_set, 1)

            def inv_std(n):
                pool.wait_ge(moments, n * 2 + 2)
                if not (isinstance(n, int) and n == 0):
                    pool.wait_ge(normed, n)
                pool.tensor_tensor(minus_mean[:, :], mv[:, :, 0], minus_one[:, :], ALU.mult)
                pool.tensor_tensor(var_eps[:, :], mv[:, :, 1], eps[:, :], ALU.add)\
                    .then_inc(eps_added, 1)
                pool.wait_ge(eps_added, n + 1)
                pool.tensor_tensor(rstd[:, :], var_eps[:, :], minus_half[:, :], ALU.pow).then_inc(rstd_ready, 1)
                pool.wait_ge(rstd_ready, n + 1)
                pool.tensor_tensor(offset[:, :], minus_mean[:, :], rstd[:, :], ALU.mult).then_inc(offset_ready, 1)

            def add_bias(u, n, row):
                pool.wait_ge(normed, n + 1)
                h = hid[:, bass.ds(u * U, U), :]
                pool.tensor_tensor(h, h, row[:, :].unsqueeze(1).to_broadcast([P, U, D]), ALU.add)\
                    .then_inc(bias_added, 1)

            def weight_of(u, par):
                pool.wait_ge(rest_exp_ready, u + 1)
                if not (isinstance(u, int) and u < 2):
                    pool.wait_ge(p_ready, u * U - U)
                pool.tensor_tensor(weight[par][:, :, :].rearrange("p b q -> p (b q)"), mix[:, :], rest_exp[:, :],
                                   ALU.mult).then_inc(weight_ready, 1)

            def adjacency_rest(u):
                pool.wait_ge(mix_ready, u + 1)
                pool.tensor_tensor(adj_rest[:, :], adjT[:, :], adjT_hi[:, :], ALU.subtract)\
                    .then_inc(rest_ready, 1)

            def part_of_p(u, j):
                if j == 3:
                    pool.wait_ge(p_lo_ready, u * U + 3)
                pool.wait_ge(p_hi_ready, u * U + j + 1)
                pool.tensor_tensor(p_lo[j % 2], p32[j % 2], p_hi[j % 2], ALU.subtract).then_inc(p_lo_ready, 1)

            inv_std(0)
            inv_std(1)
            pool.wait_ge(small_loaded, 80)
            add_bias(0, 0, bo_row)
            adjacency_rest(0)
            weight_of(0, 0)
            add_bias(1, 1, bo_row)

            def unit(u, par, nxt=True, ahead=True):
                part_of_p(u, 0)
                if nxt:
                    inv_std(u + 2)
                    adjacency_rest(u + 1)
                part_of_p(u, 1)
                if nxt:
                    weight_of(u + 1, 1 - par)
                part_of_p(u, 3)
                if ahead:
                    add_bias(u + 2, u + 2, bo_row)
                elif nxt:
                    add_bias(0, UNITS, bf2_row)

            unit(0, 0)
            with pool.Fori(0, UNITS // 2 - 2) as i:
                u = i * 2 + 1
                unit(u, 1)
                unit(u + 1, 0)
            unit(UNITS - 3, 1)
            unit(UNITS - 2, 0, ahead=False)
            unit(UNITS - 1, 1, nxt=False, ahead=False)

            with pool.Fori(1, UNITS) as w:
                inv_std(w + UNITS)
                add_bias(w, w + UNITS, bf2_row)

        @block.scalar
        def _(act):
            for n, src in enumerate((Wq, Wk, Wv, Wo)):
                act.dma_start(raw[:, n, :, :], src.rearrange("(c p) n -> p c n", p=P)).then_inc(w_loaded[n], 16)

            def normalise(u, n, js):
                if js[0] == 0:
                    act.wait_ge(offset_ready, n + 1)
                    if not (isinstance(n, int) and n == 0):
                        act.wait_ge(norm_T, n * 2)
                for j in js:
                    ins = act.activation(nrm[:, j, :], hid[:, bass.ds(u * U + j, 1), :].rearrange("p a n -> p (a n)"),
                                         ACT.Identity, bias=offset[:, j:j + 1], scale=rstd[:, j:j + 1])
                if js[-1] == U - 1:
                    ins.then_inc(normed, 1)

            def norm_hi(n, c, bank):
                act.wait_ge(norm_T, n * 2 + c + 1)
                act.activation(nT_hi[:, c, :], bank[:, :], ACT.Copy).then_inc(norm_T_hi, 1)

            def adjacency(u, par):
                act.wait_ge(adj_T, u + 1)
                if not (isinstance(u, int) and u == 0):
                    act.wait_ge(rest_ready, u)
                act.activation(adjT[:, :], front_bank(par, 2)[:, :], ACT.Copy).then_inc(adjT_ready, 1)

            def adjacency_hi(u, par):
                act.activation(adj_hi[par][:, :, :].rearrange("p b k -> p (b k)"),
                               adj_sb[:, :, :].rearrange("p b k -> p (b k)"), ACT.Copy).then_inc(adj_hi_ready, 1)

            def adjacency_parts(u):
                if not (isinstance(u, int) and u == 0):
                    act.wait_ge(weight_ready, u)
                act.wait_ge(adjT_ready, u + 1)
                act.activation(adjT_hi[:, :], adjT[:, :], ACT.Copy)
                act.activation(mix[:, :], adjT[:, :], ACT.Identity, bias=quarter[:, :], scale=0.75)\
                    .then_inc(mix_ready, 1)

            def adjacency_rest(u):
                act.wait_ge(rest_ready, u + 1)
                act.activation(rest_exp[:, :], adj_rest[:, :], ACT.Exp, scale=2.0).then_inc(rest_exp_ready, 1)

            def qk_part(u, par, m):
                if m % 2 == 0 and not (isinstance(u, int) and u == 0):
                    act.wait_ge((q_stacked, k_stacked)[m // 2], u * 3 * HC * 16)
                act.wait_ge(qk, u * 4 + m + 1)
                dst = (qT, kT)[m // 2][:, 0, m % 2, :]
                act.activation(dst, front_bank(par, 3 + m)[:, :], ACT.Identity,
                               bias=bias_folded[:, m:m + 1]).then_inc(qk_hi, 1)

            def val_part(u, par, m):
                act.wait_ge(val, u * 2 + m + 1)
                act.activation(v[par][0][:, 2 * m:2 * m + 2, :, 0:HD].rearrange("p b h d -> p (b h) d"),
                               front_bank(par, 7 + m)[:, :].rearrange("p (g d) -> p g d", d=HD),
                               ACT.Copy).then_inc(val_hi, 1)

            def piece(u, par, k):
                if k < 2:
                    norm_hi(u, k, front_bank(par, k))
                elif k == 2:
                    adjacency(u, par)
                elif k < 7:
                    qk_part(u, par, k - 3)
                    if k == 5:
                        adjacency_hi(u, par)
                    if k == 6:
                        adjacency_parts(u)
                else:
                    val_part(u, par, k - 7)

            def part_of_p(b, s):
                act.wait_ge(p_ready, b + 1)
                if not (isinstance(b, int) and b < 2):
                    act.wait_ge(mixed_done, b - 1)
                act.activation(p_hi[s], p32[s], ACT.Copy).then_inc(p_hi_ready, 1)

            def att_part(p):
                act.wait_ge(att_T, p + 1)
                act.activation(aT_hi[:, :, :].rearrange("p c t -> p (c t)"), back[:, :], ACT.Copy)\
                    .then_inc(att_T_hi, 1)

            def exponent(b, s):
                act.wait_ge(logit_done, b + 1)
                if not (isinstance(b, int) and b < 2):
                    act.wait_ge(p_ready, b - 1)
                act.activation(e32[s], logit[:, :], ACT.Exp, scale=EXP_SCALE).then_inc(exp_ready, 1)

            def guard(b, s):
                if not (isinstance(b, int) and b < 2):
                    act.wait_ge(mixed_done, b - 1)
                act.activation(e_guard[s], logit[:, :], ACT.Exp, bias=log_guard[:, :], scale=EXP_SCALE)\
                    .then_inc(guard_ready, 1)

            def weight_hi(n, dst, src, gain):
                act.wait_ge(w_loaded[n], 16)
                if isinstance(gain, float):
                    ins = act.activation(dst[:, :, :], src, ACT.Copy, scale=gain)
                else:
                    for c in range(DC):
                        ins = act.activation(dst[:, c, :], src[:, c, :], ACT.Copy, scale=gain[:, c:c + 1])
                ins.then_inc(w_hi_made, 1)

            act.wait_ge(gains_set, 1)
            weight_hi(0, w_qkvo["q"][0], raw[:, 0, :, :], gain_q)
            weight_hi(1, w_qkvo["k"][0], raw[:, 1, :, :], gain_kv)
            weight_hi(2, w_qkvo["v"][0], raw[:, 2, :, :], gain_kv)
            normalise(0, 0, range(U))
            for k in range(3):
                piece(0, 0, k)
            act.wait_ge(bias_ready, 1)
            for k in range(3, 7):
                piece(0, 0, k)
            weight_hi(3, w_qkvo["o"][0], raw[:, 3, :, :], WS)
            piece(0, 0, 7)
            act.wait_ge(gains_set, 2)
            weight_hi(4, wf1_hi, raw_f1, gain_f1)
            piece(0, 0, 8)
            normalise(1, 1, range(U))
            adjacency_rest(0)
            for k in range(3):
                piece(1, 1, k)
            weight_hi(5, wf2_hi, raw_f2, WS)
            piece(1, 1, 3)
            piece(1, 1, 4)

            def unit(u, par, first=False, last=2):
                for j in range(U):
                    b = u * U + j
                    exponent(b, j % 2)
                    if j == 2 and last > 0:
                        normalise(u + 2 if last > 1 else 0, u + 2, (2, 3))
                    guard(b, j % 2)
                    if j == 1 and last > 0:
                        normalise(u + 2 if last > 1 else 0, u + 2, (0,))
                    if j == 3 and last > 0:
                        adjacency_rest(u + 1)
                    if j == 3 and last > 1:
                        piece(u + 2, par, 2)
                    part_of_p(b, j % 2)
                    if j == 1 and not first:
                        att_part(u * 2 - 1)
                    if j == 3:
                        att_part(u * 2)
                    for n, buffers, k in ahead_of(u, par, j, last):
                        if k != 2:
                            piece(n, buffers, k)
                    if j == 1 and last > 0:
                        normalise(u + 2 if last > 1 else 0, u + 2, (1,))

            unit(0, 0, first=True)
            with act.Fori(0, UNITS // 2 - 2) as i:
                u = i * 2 + 1
                unit(u, 1)
                unit(u + 1, 0)
            unit(UNITS - 3, 1)
            unit(UNITS - 2, 0, last=1)
            unit(UNITS - 1, 1, last=0)

            def gelu(w, f):
                act.wait_ge(ff1_done, w * FC + f + 1)
                if f >= 4 or not (isinstance(w, int) and w == 0):
                    act.wait_ge(h_lo_ready, w * FC + f - 3)
                if f == 0 and not (isinstance(w, int) and w == 0):
                    act.wait_ge(ff2_done, w * 2)
                act.activation(h32[:, f % 4, :], hbank[f % 4], ACT.Gelu,
                               bias=bias_folded[:, 4 + f:5 + f], scale=1.0 / WS).then_inc(gelu_done, 1)
                act.wait_ge(gelu_done, w * FC + f + 1)
                act.activation(h_hi[:, f, :], h32[:, f % 4, :], ACT.Copy).then_inc(h_hi_ready, 1)

            def ff_unit(w, nxt=True):
                for f in range(FC):
                    if isinstance(w, int) and w == 0 and f == 4:
                        att_part(B // 2 - 1)
                    gelu(w, f)
                if nxt:
                    normalise(w + 1, w + UNITS + 1, range(U))
                    norm_hi(w + UNITS + 1, 0, front[0])
                    norm_hi(w + UNITS + 1, 1, front[1])

            act.wait_ge(f1_bias_ready, 1)
            ff_unit(0)
            with act.Fori(1, UNITS - 1) as w:
                ff_unit(w)
            ff_unit(UNITS - 1, nxt=False)

        @block.tensor
        def _(pe):
            def shift_times(dst, w, shift_col, cols):
                for k in range(DC):
                    mm = pe.matmul(dst, w[:, k, cols], ln_cols[:, shift_col, k:k + 1],
                                   start=(k == 0), stop=(k == DC - 1))
                return mm

            def chunk(f):
                return slice(f * P, (f + 1) * P)

            pe.wait_ge(gain1_loaded, 32)
            for n in range(4):
                pe.wait_ge(w_loaded[n // 2], 16)
                shift_times(mixed[:, n:n + 1], raw[:, n // 2, :, :], 1, chunk(n % 2))
            pe.wait_ge(w_loaded[2], 16)
            for k in range(DC):
                mm = pe.matmul(back[:, 0:D], ln_cols[:, 1, k:k + 1].to_broadcast([P, P]), raw[:, 2, k, :],
                               start=(k == 0), stop=(k == DC - 1))
            mm.then_inc(bias_made, 1)
            pe.wait_ge(ident_set, 2)

            def products(parts):
                return [(l, r) for lh, ll, rh, rl in parts for l, r in ((lh, rh), (lh, rl), (ll, rh))]

            def accumulate(dst, pairs):
                for n, (lhs, rhs) in enumerate(pairs):
                    mm = pe.matmul(dst, lhs, rhs, start=(n == 0), stop=(n == len(pairs) - 1))
                return mm

            def norm_transposes(n, c, bank):
                if c == 0:
                    pe.wait_ge(normed, n + 1)
                for j in range(U):
                    mm = pe.transpose(bank[:, j * P:(j + 1) * P], nrm[:, j, c * P:(c + 1) * P], ident[:, :])
                mm.then_inc(norm_T, 1)

            def piece(u, par, k):
                bank = front_bank(par, k)
                if k < 2:
                    if not (isinstance(u, int) and u == 0):
                        pe.wait_ge(val_lo, u * 2 - 1 + k)
                    norm_transposes(u, k, bank)
                elif k == 2:
                    pe.wait_ge(norm_T_lo, u * 2 + 1)
                    pe.wait_ge(adj_loaded, u * 16 + 16)
                    for j in range(U):
                        mm = pe.transpose(bank[:, j * P:(j + 1) * P], adj_sb[:, j, :], ident[:, :])
                    mm.then_inc(adj_T, 1)
                elif k < 7:
                    m = k - 3
                    if m == 0:
                        pe.wait_ge(norm_T_lo, u * 2 + 2)
                    elif m == 1:
                        pe.wait_ge(adjT_ready, u + 1)
                    else:
                        pe.wait_ge(qk_lo, u * 4 + m - 1)
                    w_hi, w_lo = w_qkvo["qk"[m // 2]]
                    cols = slice((m % 2) * P, (m % 2 + 1) * P)
                    accumulate(bank[:, :],
                               products([(w_hi[:, c, cols], w_lo[:, c, cols], nT_hi[:, c, :], nT_lo[:, c, :])
                                         for c in range(DC)])).then_inc(qk, 1)
                else:
                    m = k - 7
                    pe.wait_ge(qk_lo, u * 4 + 3 + m)
                    w_hi, w_lo = w_qkvo["v"]
                    for jj in range(2):
                        tok = slice((2 * m + jj) * P, (2 * m + jj + 1) * P)
                        mm = accumulate(bank[:, jj * D:(jj + 1) * D],
                                        products([(nT_hi[:, c, tok], nT_lo[:, c, tok], w_hi[:, c, :], w_lo[:, c, :])
                                                  for c in range(DC)]) + [(bv_pick[:, :], bv_parts[:, :])])
                    mm.then_inc(val, 1)

            def row_logits(u, j, par):
                b = u * U + j
                if j == 0:
                    pe.wait_ge(q_stacked, (u + 1) * 3 * HC * 16)
                    pe.wait_ge(k_stacked, (u + 1) * 3 * HC * 16)
                if not (isinstance(b, int) and b == 0):
                    pe.wait_ge(shift_ready, b)
                tok = slice(j * P, (j + 1) * P)
                for h in range(H):
                    c, r = divmod(h, HC)
                    mm = pe.matmul(row_logit[:, h * P:(h + 1) * P], stack[0:3 * HD, par, 0, c, r, tok],
                                   stack[0:3 * HD, par, 1, c, r, tok], start=True, stop=True)
                mm.then_inc(row_done, 1)

            def logits(u, j, par):
                b = u * U + j
                if not (isinstance(b, int) and b == 0):
                    pe.wait_ge(guard_ready, b)
                if j == 0:
                    pe.wait_ge(adj_hi_ready, u + 1)
                tok = slice(j * P, (j + 1) * P)
                for c in range(DC):
                    pe.matmul(logit[:, c * HC * P:(c + 1) * HC * P].rearrange("p (r q) -> p r q", q=P),
                              adj_hi[par][:, j, :], two_ident[:, :].unsqueeze(1).to_broadcast([P, HC, P]),
                              start=True, stop=False)
                    for r in range(HC):
                        h = c * HC + r
                        pe.matmul(logit[:, h * P:(h + 1) * P], stack[0:3 * HD, par, 1, c, r, tok],
                                  stack[0:3 * HD, par, 0, c, r, tok], start=False, stop=False)
                pe.wait_ge(shift_ready, b + 1)
                for h in range(H):
                    mm = pe.matmul(logit[:, h * P:(h + 1) * P], shift[:, h:h + 1].to_broadcast([P, P]),
                                   ident_bf[:, :], start=False, stop=(h % HC == HC - 1))
                mm.then_inc(logit_done, 1)

            def mix_values(b, j, par, check_v):
                pe.wait_ge(guard_ready, b + 1)
                pe.wait_ge(p_lo_ready, b + 1)
                if check_v is not None:
                    pe.wait_ge(val_lo, check_v)
                if not (isinstance(b, int) and b == 0):
                    pe.wait_ge(att_ready, b)
                s = j % 2
                v_hi, v_lo = v[par]
                for h in range(H):
                    cols = slice(h * P, (h + 1) * P)
                    accumulate(mixed[:, h * VW:h * VW + HD + 1],
                               [(p_hi[s][:, cols], v_hi[:, j, h, 0:HD + 1]), (p_hi[s][:, cols], v_lo[:, j, h, 0:HD + 1]),
                                (p_lo[s][:, cols], v_hi[:, j, h, 0:HD + 1])])
                for h in range(H):
                    mm = pe.matmul(mixed[:, h * VW + HD + 1:(h + 1) * VW], e_guard[s][:, h * P:(h + 1) * P],
                                   ones_col[:, 0:1], start=True, stop=True)
                mm.then_inc(mixed_done, 1)

            def att_transposes(p, s):
                pe.wait_ge(att_ready, p * 2 + 2)
                if not (isinstance(p, int) and p == 0):
                    pe.wait_ge(resid_done, p)
                for c in range(DC):
                    for jj in range(2):
                        mm = pe.transpose(back[:, (c * 2 + jj) * P:(c * 2 + jj + 1) * P],
                                          att[:, s + jj, c * P:(c + 1) * P], ident[:, :])
                mm.then_inc(att_T, 1)

            def project(p):
                pe.wait_ge(att_T_lo, p + 1)
                w_hi, w_lo = w_qkvo["o"]
                for jj in range(2):
                    tok = slice(jj * P, (jj + 1) * P)
                    mm = accumulate(back[:, jj * D:(jj + 1) * D],
                                    products([(aT_hi[:, c, tok], aT_lo[:, c, tok], w_hi[:, c, :], w_lo[:, c, :])
                                              for c in range(DC)]))
                mm.then_inc(proj_done, 1)

            for k in range(9):
                if k in (3, 5, 7):
                    pe.wait_ge(w_made, (k - 1) // 2)
                piece(0, 0, k)
            pe.wait_ge(small_loaded, 80)
            pe.wait_ge(w_loaded[4], 16)
            pe.wait_ge(bias_ready, 1)
            for f in range(FC):
                mm = shift_times(mixed[:, f:f + 1], raw_f1, 3, chunk(f))
            mm.then_inc(f1_bias_made, 1)
            for k in range(5):
                piece(1, 1, k)
            row_logits(0, 0, 0)
            pe.wait_ge(w_made, 4)

            def unit(u, par, first=False, last=2):
                for j in range(U):
                    b = u * U + j
                    logits(u, j, par)
                    if j < U - 1:
                        row_logits(u, j + 1, par)
                    if j > 0:
                        mix_values(b - 1, j - 1, par, u * 2 + 2 if j == 1 else None)
                    elif not first:
                        mix_values(b - 1, U - 1, 1 - par, None)
                    if j == 0 and not first:
                        project(u * 2 - 2)
                    if j == 1 and not first:
                        att_transposes(u * 2 - 1, 2)
                    if j == 2 and not first:
                        project(u * 2 - 1)
                    if j == 3:
                        att_transposes(u * 2, 0)
                    for n, buffers, k in ahead_of(u, par, j, last):
                        piece(n, buffers, k)
                        if k == 2:
                            row_logits(u + 1, 0, 1 - par)
                    if j == 3 and last == 1:
                        row_logits(u + 1, 0, 1 - par)

            unit(0, 0, first=True)
            with pe.Fori(0, UNITS // 2 - 2) as i:
                u = i * 2 + 1
                unit(u, 1)
                unit(u + 1, 0)
            unit(UNITS - 3, 1)
            unit(UNITS - 2, 0, last=1)
            unit(UNITS - 1, 1, last=0)

            def ff1(w, f):
                if f >= 4 or not (isinstance(w, int) and w == 0):
                    pe.wait_ge(gelu_done, w * FC + f - 3)
                cols = slice(f * P, (f + 1) * P)
                accumulate(hbank[f % 4],
                           products([(wf1_hi[:, c, cols], wf1_lo[:, c, cols], nT_hi[:, c, :], nT_lo[:, c, :])
                                     for c in range(DC)])).then_inc(ff1_done, 1)

            def ff2(w, m):
                if m == 0 and not (isinstance(w, int) and w == 0):
                    pe.wait_ge(out_ready, w * 2 - 1)
                if m == 1 and not (isinstance(w, int) and w == 0):
                    pe.wait_ge(out_ready, w * 2)
                for jj in range(2):
                    tok = slice((2 * m + jj) * P, (2 * m + jj + 1) * P)
                    for f in range(FC):
                        if m == 0 and jj == 0:
                            pe.wait_ge(h_lo_ready, w * FC + f + 1)
                        for n, (lhs, rhs) in enumerate(products(
                                [(h_hi[:, f, tok], h_lo[:, f, tok], wf2_hi[:, f, :], wf2_lo[:, f, :])])):
                            mm = pe.matmul(obank[m][:, jj * D:(jj + 1) * D], lhs, rhs,
                                           start=(f == 0 and n == 0), stop=(f == FC - 1 and n == 2))
                mm.then_inc(ff2_done, 1)

            def ff_unit(w, nxt=True):
                if not (isinstance(w, int) and w == 0):
                    pe.wait_ge(norm_T_lo, w * 2 + 2 * UNITS + 2)
                    for f in range(FC):
                        ff1(w, f)
                ff2(w, 0)
                if nxt:
                    norm_transposes(w + UNITS + 1, 0, front[0])
                    norm_transposes(w + UNITS + 1, 1, front[1])
                if isinstance(w, int) and w == 0:
                    pe.wait_ge(resid_done, B // 2)
                ff2(w, 1)

            pe.wait_ge(norm_T_lo, 2 * UNITS + 2)
            pe.wait_ge(w_made, 6)
            pe.wait_ge(shift_ready, B)
            ff1(0, 0)
            ff1(0, 1)
            project(B // 2 - 2)
            pe.wait_ge(guard_ready, B)
            ff1(0, 2)
            ff1(0, 3)
            mix_values(B - 1, U - 1, 1, None)
            att_transposes(B // 2 - 1, 2)
            ff1(0, 4)
            ff1(0, 5)
            project(B // 2 - 1)
            ff1(0, 6)
            ff1(0, 7)
            pe.wait_ge(att_ready, B)
            ff_unit(0)
            with pe.Fori(1, UNITS - 1) as w:
                ff_unit(w)
            ff_unit(UNITS - 1, nxt=False)

        @block.vector
        def _(dve):
            dve.memset(quarter[:, :], 0.25)
            dve.memset(log_guard[:, :], math.log(GUARD))
            dve.memset(ones_col[:, :], 1.0)
            for p in range(2):
                dve.memset(v[p][0][:, :, :, HD:VW], 1.0)
                dve.memset(v[p][1][:, :, :, HD:VW], 0.0)
            dve.wait_ge(ident_set, 2)
            dve.tensor_copy(ident_bf[:, :], ident[:, :])
            dve.tensor_scalar(two_ident[:, :], ident[:, :], 2.0 / EXP_SCALE, None, ALU.mult)
            dve.wait_ge(consts_set, 1)
            dve.memset(bv_pick[0:1, :], 1.0)
            dve.memset(bv_pick[32:33, :], 1.0)

            def stats(u, n, half):
                for j in (2 * half, 2 * half + 1):
                    ins = dve.bn_stats(bn[:, j, :], hid[:, bass.ds(u * U + j, 1), :].rearrange("p a n -> p (a n)"))
                ins.then_inc(stats_done, 1)

            def aggregate(half):
                for j in (2 * half, 2 * half + 1):
                    ins = dve.bn_aggr(mv[:, j, :], bn[:, j, :])
                ins.then_inc(moments, 1)

            dve.wait_ge(x_loaded, 16)
            stats(0, 0, 0)
            dve.wait_ge(stats_done, 1)
            aggregate(0)
            stats(0, 0, 1)
            dve.wait_ge(stats_done, 2)
            aggregate(1)

            dve.wait_ge(gain1_loaded, 32)
            dve.tensor_scalar(gain_q[:, :], ln_cols[:, 0, :], QS, None, ALU.mult)
            dve.tensor_scalar(gain_kv[:, :], ln_cols[:, 0, :], WS, None, ALU.mult).then_inc(gains_set, 1)
            dve.wait_ge(gains_set, 1)

            def weight_lo(n, hi, lo, src, gain):
                dve.wait_ge(w_hi_made, n + 1)
                if isinstance(gain, float):
                    ins = dve.scalar_tensor_tensor(lo[:, :, :], src, gain, hi[:, :, :], ALU.mult, ALU.subtract)
                else:
                    for c in range(DC):
                        ins = dve.scalar_tensor_tensor(lo[:, c, :], src[:, c, :], gain[:, c:c + 1], hi[:, c, :],
                                                       ALU.mult, ALU.subtract)
                ins.then_inc(w_made, 1)

            weight_lo(0, *w_qkvo["q"], raw[:, 0, :, :], gain_q)
            weight_lo(1, *w_qkvo["k"], raw[:, 1, :, :], gain_kv)

            dve.wait_ge(bias_loaded, 48)
            dve.wait_ge(bias_made, 1)
            dve.tensor_tensor(bias_folded[:, 0:4], mixed[:, 0:4], bias_cols[:, 0:4], ALU.add)
            dve.tensor_tensor(bv_row[:, :], back[:, 0:D], bv_row[:, :], ALU.add).then_inc(bias_sum, 1)
            dve.wait_ge(bias_sum, 1)
            dve.tensor_scalar(bias_folded[:, 0:2], bias_folded[:, 0:2], QS, None, ALU.mult)
            dve.tensor_scalar(bias_folded[:, 2:4], bias_folded[:, 2:4], WS, None, ALU.mult)
            dve.tensor_scalar(bv_row[:, :], bv_row[:, :], WS, None, ALU.mult).then_inc(bias_sum, 1)
            dve.wait_ge(bias_sum, 2)
            dve.tensor_copy(bv_parts[:, :], bv_row[:, :]).then_inc(bias_sum, 1)
            dve.wait_ge(bias_sum, 3)
            dve.tensor_tensor(bv_parts[32:64, :], bv_row[32:64, :], bv_parts[32:64, :], ALU.subtract)\
                .then_inc(bias_ready, 1)

            def norm_lo(n, c, bank):
                dve.wait_ge(norm_T_hi, n * 2 + c + 1)
                dve.tensor_tensor(nT_lo[:, c, :], bank[:, :], nT_hi[:, c, :], ALU.subtract)\
                    .then_inc(norm_T_lo, 1)

            def qk_part(u, par, m):
                dve.wait_ge(qk_hi, u * 4 + m + 1)
                hi, lo = [(qT, kT)[m // 2][:, part, m % 2, :] for part in range(2)]
                dve.scalar_tensor_tensor(lo, front_bank(par, 3 + m)[:, :], bias_folded[:, m:m + 1], hi,
                                         ALU.add, ALU.subtract).then_inc(qk_lo, 1)

            def val_part(u, par, m):
                dve.wait_ge(val_hi, u * 2 + m + 1)
                part = [v[par][i][:, 2 * m:2 * m + 2, :, 0:HD].rearrange("p b h d -> p (b h) d") for i in range(2)]
                dve.tensor_tensor(part[1], front_bank(par, 7 + m)[:, :].rearrange("p (g d) -> p g d", d=HD), part[0],
                                  ALU.subtract).then_inc(val_lo, 1)

            def piece(u, par, k):
                if k < 2:
                    norm_lo(u, k, front_bank(par, k))
                elif k == 2:
                    pass
                elif k < 7:
                    qk_part(u, par, k - 3)
                else:
                    val_part(u, par, k - 7)

            def maximum(b):
                dve.wait_ge(row_done, b + 1)
                if not (isinstance(b, int) and b == 0):
                    dve.wait_ge(logit_done, b)
                dve.tensor_reduce(shift[:, :], row_logit[:, :].rearrange("p (h k) -> p h k", k=P), AX.X, ALU.max,
                                  negate=True).then_inc(shift_ready, 1)

            def weighted(u, j, par):
                b = u * U + j
                dve.wait_ge(exp_ready, b + 1)
                if j == 0:
                    dve.wait_ge(weight_ready, u + 1)
                if not (isinstance(b, int) and b < 2):
                    dve.wait_ge(p_lo_ready, b - 1)
                dve.tensor_tensor(p32[j % 2].rearrange("p (h q) -> p h q", q=P),
                                  e32[j % 2].rearrange("p (h q) -> p h q", q=P),
                                  graph(weight[par], j), ALU.mult).then_inc(p_ready, 1)

            def part_of_p(b, s):
                dve.wait_ge(p_lo_ready, b)
                dve.wait_ge(p_hi_ready, b + 1)
                dve.tensor_tensor(p_lo[s], p32[s], p_hi[s], ALU.subtract).then_inc(p_lo_ready, 1)

            per_head = mixed[:, 0:H * VW].rearrange("p (h d) -> p h d", d=VW)

            def denominator(b):
                dve.wait_ge(mixed_done, b + 1)
                dve.tensor_reduce(denom[:, :], per_head[:, :, HD:VW], AX.X, ALU.max).then_inc(denom_ready, 1)

            def reciprocal(b):
                dve.wait_ge(denom_ready, b + 1)
                dve.reciprocal(recip[:, :], denom[:, :]).then_inc(recip_ready, 1)

            def attended(b, j, transposed):
                dve.wait_ge(recip_ready, b + 1)
                if transposed is not None and j % 2 == 0:
                    dve.wait_ge(att_T, transposed)
                dve.tensor_tensor(att[:, j, :].rearrange("p (h d) -> p h d", d=HD), per_head[:, :, 0:HD],
                                  recip[:, :].unsqueeze(2).to_broadcast([P, H, HD]), ALU.mult)\
                    .then_inc(att_ready, 1)

            def att_part(p):
                dve.wait_ge(att_T_hi, p + 1)
                dve.tensor_tensor(aT_lo[:, :, :].rearrange("p c t -> p (c t)"), back[:, :],
                                  aT_hi[:, :, :].rearrange("p c t -> p (c t)"), ALU.subtract).then_inc(att_T_lo, 1)

            def residual(p, b):
                dve.wait_ge(proj_done, p + 1)
                h = hid[:, bass.ds(b, 2), :].rearrange("p a n -> p (a n)")
                dve.scalar_tensor_tensor(h, back[:, :], 1.0 / (WS * WS), h, ALU.mult, ALU.add)\
                    .then_inc(resid_done, 1)

            piece(0, 0, 0)
            piece(0, 0, 1)
            weight_lo(2, *w_qkvo["v"], raw[:, 2, :, :], gain_kv)
            piece(0, 0, 3)
            dve.wait_ge(x_loaded, 32)
            dve.wait_ge(offset_ready, 1)
            stats(1, 1, 0)
            piece(0, 0, 4)
            stats(1, 1, 1)
            piece(0, 0, 5)
            dve.wait_ge(stats_done, 4)
            aggregate(0)
            aggregate(1)
            piece(0, 0, 6)
            weight_lo(3, *w_qkvo["o"], raw[:, 3, :, :], WS)
            dve.wait_ge(small_loaded, 80)
            dve.tensor_scalar(gain_f1[:, :], ln_cols[:, 2, :], WS, None, ALU.mult).then_inc(gains_set, 1)
            piece(0, 0, 7)
            dve.wait_ge(gains_set, 2)
            weight_lo(4, wf1_hi, wf1_lo, raw_f1, gain_f1)
            piece(0, 0, 8)
            dve.wait_ge(f1_bias_made, 1)
            dve.tensor_tensor(bias_folded[:, 4:4 + FC], mixed[:, 0:FC], bias_cols[:, 4:4 + FC], ALU.add)\
                .then_inc(f1_bias_ready, 1)
            piece(1, 1, 0)
            piece(1, 1, 1)
            weight_lo(5, wf2_hi, wf2_lo, raw_f2, WS)
            piece(1, 1, 3)
            piece(1, 1, 4)
            maximum(0)
            dve.wait_ge(x_loaded, 48)
            stats(2, 2, 0)
            stats(2, 2, 1)

            def unit(u, par, first=False, last=3):
                for j in range(U):
                    b = u * U + j
                    before = not (first and j == 0)
                    if j == 0 and last > 0:
                        dve.wait_ge(offset_ready, u + 2)
                        dve.wait_ge(stats_done, u * 2 + 6)
                    weighted(u, j, par)
                    if j == 0 and last > 0:
                        aggregate(0)
                        aggregate(1)
                    if before:
                        denominator(b - 1)
                    if last > 0 or j < U - 1:
                        maximum(b + 1)
                    if before:
                        reciprocal(b - 1)
                    if before:
                        attended(b - 1, (j - 1) % U, None if first else u * 2 - 1 + j // 2)
                    if j == 2:
                        part_of_p(b, 0)
                    if j == 0 and not first:
                        dve.wait_ge(bias_added, u)
                        residual(u * 2 - 2, u * U - U)
                    if j == 1 and not first:
                        att_part(u * 2 - 1)
                    if j == 2 and not first:
                        residual(u * 2 - 1, u * U - 2)
                    if j == 3:
                        att_part(u * 2)
                    for n, buffers, k in ahead_of(u, par, j, last):
                        piece(n, buffers, k)
                    if j == 3 and last == 3:
                        dve.wait_ge(x_loaded, u * 16 + 64)
                        stats(u + 3, u + 3, 0)
                        stats(u + 3, u + 3, 1)
                    if j == 3 and last == 2:
                        dve.wait_ge(resid_done, 2)
                        stats(0, UNITS, 0)
                        stats(0, UNITS, 1)

            unit(0, 0, first=True)
            with dve.Fori(0, UNITS // 2 - 2) as i:
                u = i * 2 + 1
                unit(u, 1)
                unit(u + 1, 0)
            unit(UNITS - 3, 1, last=2)
            unit(UNITS - 2, 0, last=1)
            unit(UNITS - 1, 1, last=0)

            def h_part(w, f, nxt):
                if nxt and f in (1, 3):
                    dve.wait_ge(stats_done, w * 2 + 2 * UNITS + 3 + f // 2)
                dve.wait_ge(h_hi_ready, w * FC + f + 1)
                dve.tensor_tensor(h_lo[:, f, :], h32[:, f % 4, :], h_hi[:, f, :], ALU.subtract)\
                    .then_inc(h_lo_ready, 1)

            def finish(w, m):
                dve.wait_ge(ff2_done, w * 2 + m + 1)
                dve.wait_ge(bias_added, w + UNITS + 1)
                h = hid[:, bass.ds(w * U + 2 * m, 2), :].rearrange("p a n -> p (a n)")
                dve.scalar_tensor_tensor(h, obank[m][:, :], 1.0 / WS, h, ALU.mult, ALU.add)\
                    .then_inc(out_ready, 1)

            def attention_end(f):
                if f == 0:
                    dve.wait_ge(bias_added, UNITS)
                    residual(B // 2 - 2, B - 4)
                if f == 1:
                    denominator(B - 1)
                    reciprocal(B - 1)
                    attended(B - 1, 3, None)
                if f == 3:
                    att_part(B // 2 - 1)
                if f == 5:
                    residual(B // 2 - 1, B - 2)

            def ff_unit(w, nxt=True):
                for f in range(FC):
                    if nxt and f in (0, 2):
                        if f == 0:
                            dve.wait_ge(offset_ready, w + UNITS + 1)
                        stats(w + 1, w + UNITS + 1, f // 2)
                    h_part(w, f, nxt)
                    if isinstance(w, int) and w == 0:
                        attention_end(f)
                    if nxt and f in (1, 3):
                        aggregate(f // 2)
                if nxt:
                    norm_lo(w + UNITS + 1, 0, front[0])
                    norm_lo(w + UNITS + 1, 1, front[1])
                finish(w, 0)
                finish(w, 1)

            ff_unit(0)
            with dve.Fori(1, UNITS - 1) as w:
                ff_unit(w)
            ff_unit(UNITS - 1, nxt=False)


_INS = ["x", "adj"] + ["L0_gnn_" + n for n in (
    "Wq", "bq", "Wk", "bk", "Wv", "bv", "Wo", "bo", "g1", "b1", "g2", "b2", "Wf1", "bf1", "Wf2", "bf2")]


def kernel(**inputs):
    import numpy as _np
    import concourse.bacc as _bacc
    from concourse import mybir as _mybir
    from concourse.bass_utils import run_bass_kernel_spmd as _run

    nc = _bacc.Bacc("TRN2", target_bir_lowering=False, num_devices=1)
    arrays, args = {}, []
    for name in _INS:
        a = _np.ascontiguousarray(inputs[name])
        arrays[f"in_{name}"] = a
        args.append(nc.dram_tensor(f"in_{name}", a.shape, _mybir.dt.from_np(a.dtype), kind="ExternalInput").ap())
    shape = inputs["x"].shape
    args.append(nc.dram_tensor("out", shape, _mybir.dt.float32, kind="ExternalOutput").ap())
    gnn_layer(nc, *args)
    r = _run(nc, [arrays], core_ids=[0])
    return r.results[0]["out"]
```
